# Optimizing a Trainium2 kernel written in Bass

```python
import numpy as np
import jax
import jax.numpy as jnp

def _softmax(x, axis=-1):
    return jax.nn.softmax(x, axis=axis)

def _gelu(x):
    return jax.nn.gelu(x, approximate=True)

def _silu(x):
    return jax.nn.silu(x)

def _sigmoid(x):
    return jax.nn.sigmoid(x)

def _layernorm(x, axis=-1, eps=1e-05):
    m = jnp.mean(x, axis=axis, keepdims=True)
    v = jnp.var(x, axis=axis, keepdims=True)
    return (x - m) / jnp.sqrt(v + eps)

def _scatter_add(tgt, idx, src, axis=0):
    return tgt.at[idx].add(src)

def _segment_sum(src, seg, n):
    return jax.ops.segment_sum(src, seg, n)
kernel_name = 'mk_gnn_preln_d2_gnn_r8_50e8cd'

def setup_inputs(seed: int=0):
    np.random.seed(seed)
    _w = jnp.asarray

    def _rec_inputs():
        import jax
        import jax.numpy as jnp
        _gk = jax.random.key(seed)
        x = -0.000202 + 1 * jax.random.normal(jax.random.fold_in(_gk, 1), (12500, 128), jnp.float32)
        _s = jax.random.randint(jax.random.fold_in(_gk, 2), (100000,), 0, 12500, jnp.int32)
        _d = jax.random.randint(jax.random.fold_in(_gk, 3), (100000,), 0, 12500, jnp.int32)
        _loop = jnp.arange(12500, dtype=jnp.int32)
        src = jnp.concatenate([_s, _d, _loop])
        dst = jnp.concatenate([_d, _s, _loop])
        _o = jnp.argsort(dst, stable=True)
        src = src[_o]
        dst = dst[_o]
        edge_attr_128 = -8.16379e-05 + 0.999858 * jax.random.normal(jax.random.fold_in(_gk, 12), (212500, 128), jnp.float32)
        return (x, src, dst, edge_attr_128)
    x, src, dst, edge_attr_128 = _rec_inputs()

    def _L0_gnn_setup():
        import jax, jax.numpy as jnp
        import numpy as np
        N, IN, H, D = (6250, 128, 4, 32)
        HID = H * D
        E = 100000
        key = jax.random.key(seed)
        ks = jax.random.split(key, 16)
        s_in = 1.0 / np.sqrt(IN)
        s_g = 1.0 / np.sqrt(3 * HID)
        inp = {'feat': jax.random.normal(ks[0], (N, IN), jnp.float32), 'src': jax.random.randint(ks[1], (E,), 0, N, jnp.int32), 'dst': jax.random.randint(ks[2], (E,), 0, N, jnp.int32), 'Wq': jax.random.normal(ks[3], (IN, HID), jnp.float32) * s_in, 'bq': jnp.zeros((HID,), jnp.float32), 'Wk': jax.random.normal(ks[4], (IN, HID), jnp.float32) * s_in, 'bk': jnp.zeros((HID,), jnp.float32), 'Wv': jax.random.normal(ks[5], (IN, HID), jnp.float32) * s_in, 'bv': jnp.zeros((HID,), jnp.float32), 'Ws': jax.random.normal(ks[6], (IN, HID), jnp.float32) * s_in, 'bs': jnp.zeros((HID,), jnp.float32), 'Wg': jax.random.normal(ks[7], (3 * HID, 1), jnp.float32) * s_g, 'bg': jnp.zeros((1,), jnp.float32), 'gamma': jnp.ones((HID,), jnp.float32), 'beta': jnp.zeros((HID,), jnp.float32), 'alpha': jnp.asarray(0.25, jnp.float32)}
        return inp
    _L0_gnn_all = _L0_gnn_setup()
    _L0_gnn_in = {k: v for k, v in _L0_gnn_all.items() if k in ('Wq', 'bq', 'Wk', 'bk', 'Wv', 'bv', 'Ws', 'bs', 'Wg', 'bg', 'gamma', 'beta', 'alpha')}
    del _L0_gnn_all

    def _L1_gnn_setup():
        import jax, jax.numpy as jnp
        import numpy as np
        N_NODES = 6250
        N_EDGES = 100000
        D_IN = 128
        OUT = 128
        H = 4
        D = OUT // H
        NEG_SLOPE = 0.2

        def _leaky_relu(x):
            return jnp.where(x >= 0, x, NEG_SLOPE * x)

        def _edge_softmax(e, dst, n_nodes):
            m = jax.ops.segment_max(e, dst, num_segments=n_nodes)
            m = jnp.where(jnp.isfinite(m), m, 0.0)
            ex = jnp.exp(e - m[dst])
            s = jax.ops.segment_sum(ex, dst, num_segments=n_nodes)
            return ex / s[dst]
        key = jax.random.key(seed)
        ks = jax.random.split(key, 10)
        return {'X': jax.random.normal(ks[0], (N_NODES, D_IN), dtype=jnp.float32), 'X_edge': jax.random.normal(ks[1], (N_EDGES, D_IN), dtype=jnp.float32), 'W_src': jax.random.normal(ks[2], (OUT, D_IN), dtype=jnp.float32) * 0.05, 'W_dst': jax.random.normal(ks[3], (OUT, D_IN), dtype=jnp.float32) * 0.05, 'W_edge': jax.random.normal(ks[4], (OUT, D_IN), dtype=jnp.float32) * 0.05, 'attn_src': jax.random.normal(ks[5], (H, D), dtype=jnp.float32), 'attn_dst': jax.random.normal(ks[6], (H, D), dtype=jnp.float32), 'attn_edge': jax.random.normal(ks[7], (H, D), dtype=jnp.float32), 'src': jax.random.randint(ks[8], (N_EDGES,), 0, N_NODES, dtype=jnp.int32), 'dst': jax.random.randint(ks[9], (N_EDGES,), 0, N_NODES, dtype=jnp.int32)}
    _L1_gnn_all = _L1_gnn_setup()
    _L1_gnn_in = {k: v for k, v in _L1_gnn_all.items() if k in ('W_src', 'W_dst', 'W_edge', 'attn_src', 'attn_dst', 'attn_edge')}
    del _L1_gnn_all
    return {'x': x, 'src': src, 'dst': dst, 'edge_attr_128': edge_attr_128, 'L0_gnn_Wq': _L0_gnn_in['Wq'], 'L0_gnn_bq': _L0_gnn_in['bq'], 'L0_gnn_Wk': _L0_gnn_in['Wk'], 'L0_gnn_bk': _L0_gnn_in['bk'], 'L0_gnn_Wv': _L0_gnn_in['Wv'], 'L0_gnn_bv': _L0_gnn_in['bv'], 'L0_gnn_Ws': _L0_gnn_in['Ws'], 'L0_gnn_bs': _L0_gnn_in['bs'], 'L0_gnn_Wg': _L0_gnn_in['Wg'], 'L0_gnn_bg': _L0_gnn_in['bg'], 'L0_gnn_gamma': _L0_gnn_in['gamma'], 'L0_gnn_beta': _L0_gnn_in['beta'], 'L0_gnn_alpha': _L0_gnn_in['alpha'], 'L1_gnn_W_src': _L1_gnn_in['W_src'], 'L1_gnn_W_dst': _L1_gnn_in['W_dst'], 'L1_gnn_W_edge': _L1_gnn_in['W_edge'], 'L1_gnn_attn_src': _L1_gnn_in['attn_src'], 'L1_gnn_attn_dst': _L1_gnn_in['attn_dst'], 'L1_gnn_attn_edge': _L1_gnn_in['attn_edge']}

def reference(x, src, dst, edge_attr_128, L0_gnn_Wq, L0_gnn_bq, L0_gnn_Wk, L0_gnn_bk, L0_gnn_Wv, L0_gnn_bv, L0_gnn_Ws, L0_gnn_bs, L0_gnn_Wg, L0_gnn_bg, L0_gnn_gamma, L0_gnn_beta, L0_gnn_alpha, L1_gnn_W_src, L1_gnn_W_dst, L1_gnn_W_edge, L1_gnn_attn_src, L1_gnn_attn_dst, L1_gnn_attn_edge):
    import jax
    import jax.numpy as jnp

    def _L0_gnn_ref(feat, src, dst, Wq, bq, Wk, bk, Wv, bv, Ws, bs, Wg, bg, gamma, beta, alpha):
        import jax, jax.numpy as jnp
        import numpy as np
        N, IN, H, D = (6250, 128, 4, 32)
        HID = H * D
        E = 100000
        n = feat.shape[0]
        q = (feat @ Wq + bq).reshape(n, H, D)
        k = (feat @ Wk + bk).reshape(n, H, D)
        v = (feat @ Wv + bv).reshape(n, H, D)
        a = jnp.einsum('ehd,ehd->eh', q[src], k[dst]) / jnp.sqrt(jnp.float32(D))
        m = jax.ops.segment_max(a, dst, num_segments=n)
        m = jax.lax.stop_gradient(jnp.where(jnp.isfinite(m), m, 0.0))
        ex = jnp.exp(a - m[dst])
        denom = jax.ops.segment_sum(ex, dst, num_segments=n)
        denom = jnp.where(denom > 0, denom, 1.0)
        sa = ex / denom[dst]
        msg = v[src] * sa[:, :, None]
        agg = jax.ops.segment_sum(msg, dst, num_segments=n).reshape(n, HID)
        skip = feat @ Ws + bs
        g = jax.nn.sigmoid(jnp.concatenate([skip, agg, skip - agg], axis=-1) @ Wg + bg)
        rst = g * skip + (1.0 - g) * agg
        mu = rst.mean(-1, keepdims=True)
        var = rst.var(-1, keepdims=True)
        rst = (rst - mu) * jax.lax.rsqrt(var + 1e-05) * gamma + beta
        rst = jnp.where(rst >= 0, rst, alpha * rst)
        return rst

    def _L1_gnn_ref(X, X_edge, W_src, W_dst, W_edge, attn_src, attn_dst, attn_edge, src, dst):
        import jax, jax.numpy as jnp
        import numpy as np
        N_NODES = 6250
        N_EDGES = 100000
        D_IN = 128
        OUT = 128
        H = 4
        D = OUT // H
        NEG_SLOPE = 0.2

        def _leaky_relu(x):
            return jnp.where(x >= 0, x, NEG_SLOPE * x)

        def _edge_softmax(e, dst, n_nodes):
            m = jax.ops.segment_max(e, dst, num_segments=n_nodes)
            m = jnp.where(jnp.isfinite(m), m, 0.0)
            ex = jnp.exp(e - m[dst])
            s = jax.ops.segment_sum(ex, dst, num_segments=n_nodes)
            return ex / s[dst]
        n = X.shape[0]
        h_src = (X @ W_src.T).reshape(n, H, D)
        h_dst = (X @ W_dst.T).reshape(n, H, D)
        e_src = jnp.einsum('nhd,hd->nh', h_src, attn_src)
        e_dst = jnp.einsum('nhd,hd->nh', h_dst, attn_dst)
        e = _leaky_relu(e_src[src] + e_dst[dst])
        a = _edge_softmax(e, dst, n)
        m = a[:, :, None] * h_src[src]
        h_neigh = jax.ops.segment_sum(m, dst, num_segments=n)
        h_edge = (X_edge @ W_edge.T).reshape(-1, H, D)
        e_edge = jnp.einsum('ehd,hd->eh', h_edge, attn_edge)
        e2 = _leaky_relu(e_edge + e_dst[dst])
        a2 = _edge_softmax(e2, dst, n)
        h_edge_agg = jax.ops.segment_sum(a2[:, :, None] * h_edge, dst, num_segments=n)
        h = h_dst + h_neigh + h_edge_agg
        return h.reshape(n, H * D)
    h = jnp.maximum(_layernorm(x, axis=-1), 0.0)
    x = x + _L0_gnn_ref(h, src, dst, L0_gnn_Wq, L0_gnn_bq, L0_gnn_Wk, L0_gnn_bk, L0_gnn_Wv, L0_gnn_bv, L0_gnn_Ws, L0_gnn_bs, L0_gnn_Wg, L0_gnn_bg, L0_gnn_gamma, L0_gnn_beta, L0_gnn_alpha)
    h = jnp.maximum(_layernorm(x, axis=-1), 0.0)
    x = x + _L1_gnn_ref(h, edge_attr_128, L1_gnn_W_src, L1_gnn_W_dst, L1_gnn_W_edge, L1_gnn_attn_src, L1_gnn_attn_dst, L1_gnn_attn_edge, src, dst)
    return x

_drawn_inputs = setup_inputs


def setup_inputs(seed=0):
    import zlib

    import numpy as np

    out = dict(_drawn_inputs(seed))
    spreads = {'L0_gnn_bq': (0.0, 0.8),
     'L0_gnn_bk': (0.0, 0.759),
     'L0_gnn_bv': (0.0, 0.1),
     'L0_gnn_bs': (0.0, 0.1),
     'L0_gnn_gamma': (1.0, 0.2),
     'L0_gnn_beta': (0.0, 0.1)}
    factors = {}
    for name, (base, spread) in spreads.items():
        noise = np.random.default_rng([zlib.crc32(name.encode()), seed]).standard_normal(out[name].shape)
        drawn = base * np.exp(spread * noise) if base else spread * noise
        out[name] = jnp.asarray(drawn.astype(out[name].dtype))
    for name, factor in factors.items():
        out[name] = (out[name] * factor).astype(out[name].dtype)
    return out
```

```python
from contextlib import ExitStack

import numpy as np

import concourse.bass as bass
from concourse import mybir
from concourse.alu_op_type import AluOpType as ALU

ACT = mybir.ActivationFunctionType
AX = mybir.AxisListType.X
F32 = mybir.dt.float32
I32 = mybir.dt.int32

P = 128
D = 128
H = 4
HD = D // H
GT = 4
CT = P // H
EPS = 1e-5
SLOPE = 0.2
BIG = 1e30


def sizes(n_nodes, n_edges):
    node_tiles = -(-(n_nodes + P + 1) // P)
    node_tiles += node_tiles % 2
    unit = P * P
    return node_tiles, -(-n_edges // unit) * P


def build(nc, A, n_nodes, n_edges):
    NT, ET = sizes(n_nodes, n_edges)
    NP = NT * P
    EP = ET * P
    G = ET // GT
    C = ET // CT
    ST = ET // P
    SL = ST * P
    assert G % 4 == 0 and ET * H == C * P and C % GT == 0 and NP <= 2 * ET * H and 7 * SL <= NP

    def dram(name, shape):
        return nc.dram_tensor(name, shape, F32, kind="Internal").ap()

    qv_table = dram("qv_table", (NP, 2 * D))
    k_table = dram("k_table", (NP, D))
    skip_table = dram("skip_table", (NP, D))
    hs_table = dram("hs_table", (NP, D + H))
    ed_table = dram("ed_table", (NP, H))
    gathered = dram("gathered", (G, P, GT * D))
    rows_out = dram("rows_out", (ET * H, P))
    rows_in = dram("rows_in", (ET * H, P))

    with ExitStack() as ctx:
        def sb(name, shape, dt=F32):
            return ctx.enter_context(nc.sbuf_tensor(name, shape, dt))

        phase_sems = []

        def sem(name):
            phase_sems.append(nc.alloc_semaphore(name=name))
            return phase_sems[-1]

        def phase(program, *args):
            program(*args)
            nc.clear_and_free_semaphores(phase_sems)
            nc.all_engine_barrier()
            phase_sems.clear()

        def sems(name, n):
            return [sem(f"{name}{i}") for i in range(n)]

        X = sb("X", [P, NT, D])
        SUM = sb("SUM", [P, NP])
        W = sb("W", [P, 2 * ET * H])
        W1, W2 = W[:, 0:ET * H], W[:, ET * H:2 * ET * H]
        REL = sb("REL", [P, ET + GT])
        SRC = sb("SRC", [P, ET], I32)
        SCR = sb("SCR", [P, 9472])
        ident = sb("ident", [P, P])
        iota_row = sb("iota_row", [P, P])
        psum = [ctx.enter_context(nc.psum_tensor(f"bank{i}", [P, 512], F32)) for i in range(8)]

        class Carve:
            def __init__(self):
                self.at = 0

            def __call__(self, n):
                self.at += n
                assert self.at <= SCR.shape[1], self.at
                return SCR[:, self.at - n:self.at]

        def chained(eng, s):
            count = [0]

            def link(ins):
                count[0] += 1
                ins.then_inc(s, 1)
                eng.wait_ge(s, count[0])
            return link

        def wait(eng, s, value):
            if not isinstance(value, int) or value > 0:
                eng.wait_ge(s, value)

        def done(eng, s, i, k, each=1):
            n = len(s)
            wait(eng, s[k % n], (i * (4 // n) + k // n + 1) * each)

        def loop(eng, n, body):
            body(0)
            if n > 1:
                with eng.Fori(1, n) as i:
                    body(i)

        def window_starts(eng, engine, first, i):
            return nc.values_load_multi_w_load_instructions(first[0:1, bass.ds(i * 4 * GT, 4 * GT)], engines=[engine],
                                                            min_val=0, max_val=n_nodes)[1]

        def cols(t, start, n):
            return t[:, bass.ds(start, n)]

        def setup():
            s_load, s_const, s_iota, s_first = sem("set_load"), sem("set_const"), sem("set_iota"), sem("set_first")
            s_chain = sem("set_chain")
            dst_i = SUM[:, 0:ET].bitcast(I32)
            first_i = SUM[:, ET:2 * ET].bitcast(I32)
            iota_i = SUM[:, 2 * ET:2 * ET + P].bitcast(I32)
            with nc.Block() as block:
                @block.sync
                def _(sp):
                    sp.dma_start(SRC[:, :], A["src_tiles"]).then_inc(s_load, 16)
                    sp.dma_start(dst_i, A["dst_tiles"]).then_inc(s_load, 16)
                    sp.dma_start(first_i, A["tile_first"].partition_broadcast(P)).then_inc(s_load, 16)
                    for c in range(2):
                        ts = slice(c * NT // 2, (c + 1) * NT // 2)
                        sp.dma_start(X[:, ts, :], A["x"].rearrange("(t p) d -> p t d", p=P)[:, ts, :]).then_inc(s_load, 16)
                    sp.wait_ge(s_load, 5 * 16)

                @block.gpsimd
                def _(pool):
                    pool.memset(ident[:, :], 0.0).then_inc(s_const, 1)
                    pool.iota(iota_i, pattern=[[1, P]], base=0, channel_multiplier=0).then_inc(s_iota, 1)
                    pool.wait_ge(s_const, 1)
                    pool.affine_select(out=ident[:, :], in_=ident[:, :], compare_op=ALU.not_equal, fill=1.0,
                                       base=0, pattern=[[-1, P]], channel_multiplier=1).then_inc(s_const, 1)

                @block.vector
                def _(dve):
                    link = chained(dve, s_chain)
                    dve.wait_ge(s_iota, 1)
                    link(nc.vector.tensor_copy(iota_row[:, :], iota_i))
                    link(nc.vector.memset(REL[:, ET:ET + GT], -1.0))
                    dve.wait_ge(s_load, 5 * 16)
                    link(nc.vector.tensor_tensor(REL[:, 0:ET], dst_i, first_i, ALU.subtract))

        def moments(link, st, mean, dev, var, s_var):
            link(nc.vector.tensor_tensor(mean, st[:, :, 1], st[:, :, 4], ALU.add))
            link(nc.vector.tensor_scalar(mean, mean, 0.5, None, ALU.mult))
            link(nc.vector.tensor_tensor(dev, st[:, :, 1], st[:, :, 4], ALU.subtract))
            link(nc.vector.tensor_scalar(dev, dev, 0.5, None, ALU.mult))
            link(nc.vector.tensor_tensor(dev, dev, dev, ALU.mult))
            link(nc.vector.tensor_tensor(var, st[:, :, 2], st[:, :, 5], ALU.add))
            link(nc.vector.tensor_scalar(var, var, 1.0 / D, EPS, ALU.mult, ALU.add))
            nc.vector.tensor_tensor(var, var, dev, ALU.add).then_inc(s_var, 1)

        def norm_stats(name, stats, scale_out, shift_out, tmp):
            s_stats, s_chain, s_var, s_std = (sem(f"{name}_{x}") for x in ("stats", "chain", "var", "std"))
            st = stats.rearrange("p (t k) -> p t k", k=6)
            with nc.Block() as block:
                @block.vector
                def _(dve):
                    link = chained(dve, s_chain)
                    def step_dve(i):
                        for k in range(2):
                            t = bass.ds(i * 2 + k, 1)
                            nc.vector.bn_stats(st[:, t, :].rearrange("p a k -> p (a k)"),
                                               X[:, t, :].rearrange("p a d -> p (a d)")).then_inc(s_stats, 1)
                    loop(dve, NT // 2, step_dve)
                    dve.wait_ge(s_stats, NT)
                    mean, dev, var = tmp[:, 0:NT], tmp[:, NT:2 * NT], tmp[:, 2 * NT:3 * NT]
                    moments(link, st, mean, dev, var, s_var)
                    dve.wait_ge(s_std, 1)
                    link(nc.vector.reciprocal(scale_out, var))
                    link(nc.vector.scalar_tensor_tensor(shift_out, mean, -1.0, scale_out, ALU.mult, ALU.mult))

                @block.scalar
                def _(act):
                    act.wait_ge(s_var, 1)
                    var = tmp[:, 2 * NT:3 * NT]
                    nc.scalar.activation(var, var, ACT.Sqrt).then_inc(s_std, 1)


        def node_tables(layer):
            name = f"t{layer}"
            width = 4 * D if layer == 0 else 2 * D
            carve = Carve()
            stats, tmp = carve(6 * NT), carve(3 * NT)
            scale, shift = carve(NT), carve(NT)
            weights, extra = carve(width), carve(width)
            h, hT = ([carve(D) for _ in range(2)] for _ in range(2))
            out = [carve(4 * D if layer == 0 else D + 2 * H) for _ in range(2)]
            prod = carve(2 * D)
            norm_stats(f"n{layer}", stats, scale, shift, tmp)
            s_w = sem(f"{name}_weights")
            s_h, s_T, s_hT, s_mm, s_out, s_stored, s_free = (
                sems(f"{name}_{x}", 2) for x in ("h", "T", "hT", "mm", "out", "stored", "free"))
            s_prod = sem(f"{name}_prod")
            if layer == 0:
                loads = [(weights[:, n * D:(n + 1) * D], A[w]) for n, w in enumerate(("Wq", "Wv", "Wk", "Ws"))]
                loads += [(extra[:, n * D:(n + 1) * D], A[b].partition_broadcast(P)) for n, b in enumerate(("bq", "bv", "bk", "bs"))]
                stores = lambda rows, o: [(qv_table[rows, :], o[:, 0:2 * D]), (k_table[rows, :], o[:, 2 * D:3 * D]),
                                          (skip_table[rows, :], o[:, 3 * D:4 * D])]
            else:
                loads = [(weights[:, n * D:(n + 1) * D], A[w]) for n, w in enumerate(("W_src_T", "W_dst_T"))]
                loads += [(extra[:, n * D:(n + 1) * D], A[b].rearrange("h d -> (h d)").partition_broadcast(P)) for n, b in enumerate(("attn_src", "attn_dst"))]
                stores = lambda rows, o: [(hs_table[rows, :], o[:, 0:D + H]), (ed_table[rows, :], o[:, D + H:D + 2 * H])]
            each = 16 * (3 if layer == 0 else 2)
            with nc.Block() as block:
                @block.sync
                def _(sp):
                    for to, of in loads:
                        sp.dma_start(to, of).then_inc(s_w, 16)
                    def step_sp(i):
                        for s in range(2):
                            wait(sp, s_out[s], i + 1)
                            for to, of in stores(bass.ds((i * 2 + s) * P, P), out[s]):
                                sp.dma_start(to, of).then_inc(s_stored[s], 16)
                    loop(sp, NT // 2, step_sp)
                    for s in range(2):
                        sp.wait_ge(s_stored[s], NT // 2 * each)

                @block.scalar
                def _(act):
                    def step_act(i):
                        for s in range(2):
                            t = i * 2 + s
                            wait(act, s_T[s], i)
                            nc.scalar.activation(h[s], X[:, bass.ds(t, 1), :].rearrange("p a d -> p (a d)"),
                                                 ACT.Relu, bias=cols(shift, t, 1), scale=cols(scale, t, 1)).then_inc(s_h[s], 1)
                        for s in range(2):
                            wait(act, s_T[s], i + 1)
                            wait(act, s_mm[s], i)
                            nc.scalar.copy(hT[s], psum[s][:, 0:D]).then_inc(s_hT[s], 1)
                    loop(act, NT // 2, step_act)

                @block.tensor
                def _(pe):
                    pe.wait_ge(s_w, len(loads) * 16)
                    def step_pe(i):
                        for s in range(2):
                            wait(pe, s_h[s], i + 1)
                            wait(pe, s_hT[s], i)
                            nc.tensor.transpose(psum[s][:, 0:D], h[s], ident[:, :]).then_inc(s_T[s], 1)
                        for s in range(2):
                            wait(pe, s_hT[s], i + 1)
                            wait(pe, s_free[s], i)
                            nc.tensor.matmul(psum[2 + s][:, 0:width], hT[s], weights, start=True, stop=True).then_inc(s_mm[s], 1)
                    loop(pe, NT // 2, step_pe)

                @block.vector
                def _(dve):
                    dve.wait_ge(s_w, len(loads) * 16)
                    def step_dve(i):
                        for s in range(2):
                            bank, o = psum[2 + s], out[s]
                            wait(dve, s_mm[s], i + 1)
                            wait(dve, s_stored[s], i * each)
                            if layer == 0:
                                nc.vector.tensor_tensor(o, bank[:, :], extra, ALU.add).then_inc(s_out[s], 1)
                                wait(dve, s_out[s], i + 1)
                                dve.sem_inc(s_free[s], 1)
                            else:
                                at = X[:, bass.ds(i * 2 + s, 1), :].rearrange("p a d -> p (a d)")
                                nc.vector.tensor_copy(o[:, 0:D], bank[:, 0:D])
                                nc.vector.tensor_tensor(at, at, bank[:, D:2 * D], ALU.add)
                                wait(dve, s_out[1 - s], i + s)
                                nc.vector.tensor_tensor(prod, bank[:, 0:2 * D], extra, ALU.mult).then_inc(s_free[s], 1)
                                wait(dve, s_free[s], i + 1)
                                nc.vector.tensor_reduce(o[:, D:D + 2 * H], prod.rearrange("p (a d) -> p a d", d=HD), AX, ALU.add).then_inc(s_out[s], 1)
                    loop(dve, NT // 2, step_dve)

        def pass_a(layer):
            name = f"a{layer}"
            row = 2 * D if layer == 0 else D + H
            feat = D if layer == 0 else 0
            win = D if layer == 0 else H
            table = qv_table if layer == 0 else hs_table
            wtable = k_table if layer == 0 else ed_table
            carve = Carve()
            got = [carve(GT * row) for _ in range(4)]
            window, onehot, onehotT = ([carve(GT * n) for _ in range(2)] for n in (win, P, P))
            work = [carve(GT * D if layer == 0 else 2 * GT * H) for _ in range(2)]
            index = [carve(GT).bitcast(I32) for _ in range(4)]
            xe = [carve(GT * P) for _ in range(2)] if layer == 1 else None
            if layer == 1:
                w_edge, blockdiag, w4 = carve(D), carve(H), carve(H)
            turn = carve(2)[0:1, :]
            first = SUM[0:1, 0:ET].bitcast(I32)
            s_first, s_prep, s_w4, s_zero, s_turn = (sem(f"{name}_{x}") for x in ("first", "prep", "w4", "zero", "turn"))
            s_index, s_got, s_kept, s_used = (sems(f"{name}_{x}", 4) for x in ("index", "got", "kept", "used"))
            s_win, s_hot, s_T, s_hotT, s_side, s_log = (
                sems(f"{name}_{x}", 2) for x in ("window", "onehot", "T", "onehotT", "side", "logits"))
            s_xe = sems(f"{name}_xedge", 2) if layer == 1 else None

            with nc.Block() as block:
                @block.sync
                def _(sp):
                    sp.dma_start(first, A["tile_first"]).then_inc(s_first, 16)
                    if layer == 1:
                        sp.dma_start(w_edge, A["W_edge"]).then_inc(s_prep, 16)
                        sp.wait_ge(s_zero, 1)
                        for h in range(H):
                            sp.dma_start(blockdiag[h * HD:(h + 1) * HD, h:h + 1],
                                         A["attn_edge"][h:h + 1, :].rearrange("a d -> d a")).then_inc(s_prep, 16)
                    sp.wait_ge(s_first, 16)
                    def step_sp(i):
                        starts = window_starts(sp, mybir.EngineType.SP, first, i)
                        for k in range(4):
                            g = i * 4 + k
                            done(sp, s_side, i, k - 2)
                            for j in range(GT):
                                sp.dma_start(window[k % 2][:, j * win:(j + 1) * win], wtable[bass.ds(starts[k * GT + j], P), :]).then_inc(s_win[k % 2], 16)
                            if layer == 1:
                                sp.dma_start(xe[k % 2], A["xe_T"][:, bass.ds(g * GT * P, GT * P)]).then_inc(s_xe[k % 2], 16)
                    loop(sp, G // 4, step_sp)

                @block.scalar
                def _(act):
                    def step_act(i):
                        for k in range(4):
                            done(act, s_got, i, k - 4, 16 * GT)
                            nc.scalar.copy(index[k], cols(SRC, (i * 4 + k) * GT, GT)).then_inc(s_index[k], 1)
                        for k in range(4):
                            done(act, s_T, i, k)
                            done(act, s_side, i, k - 2)
                            nc.scalar.copy(onehotT[k % 2], psum[k % 2][:, :]).then_inc(s_hotT[k % 2], 1)
                            done(act, s_got, i, k, 16 * GT)
                            kept = got[k].rearrange("p (t d) -> p t d", t=GT)[:, :, feat:feat + D]
                            to = gathered[bass.ds(i * 4 + k, 1), :, :].rearrange("a p (t d) -> (a p) t d", t=GT)
                            act.dma_start(to, kept).then_inc(s_kept[k], 16)
                    loop(act, G // 4, step_act)
                    for k in range(4):
                        act.wait_ge(s_kept[k], G // 4 * 16)

                @block.gpsimd
                def _(pool):
                    nc.gpsimd.memset(turn[:, 0:1], 0.0).then_inc(s_turn, 1)
                    pool.wait_ge(s_turn, 1)
                    def step_pool(i):
                        for k in range(4):
                            wait(pool, s_turn, i * 4 + k + 1)
                            done(pool, s_index, i, k)
                            done(pool, s_used, i, k - 4)
                            done(pool, s_kept, i, k - 4, 16)
                            nc.gpsimd.tensor_tensor(turn[:, 1:2], turn[:, 0:1], turn[:, 0:1], ALU.add).then_inc(s_turn, 1)
                            for j in range(GT):
                                pool.indirect_dma_start(out=got[k][:, j * row:(j + 1) * row], out_offset=None, in_=table,
                                                        in_offset=bass.IndirectOffsetOnAxis(ap=index[k][:, j:j + 1], axis=0)).then_inc(s_got[k], 16)
                    loop(pool, G // 4, step_pool)

                @block.tensor
                def _(pe):
                    if layer == 1:
                        pe.wait_ge(s_prep, 5 * 16)
                        nc.tensor.matmul(psum[4][:, 0:H], w_edge, blockdiag, start=True, stop=True).then_inc(s_w4, 1)
                        pe.wait_ge(s_w4, 2)

                    def transposes(i, k):
                        done(pe, s_hot, i, k)
                        done(pe, s_hotT, i, k - 2)
                        for j in range(GT):
                            last = nc.tensor.transpose(psum[k % 2][:, j * P:(j + 1) * P], onehot[k % 2][:, j * P:(j + 1) * P], ident[:, :])
                        last.then_inc(s_T[k % 2], 1)

                    def side(i, k):
                        done(pe, s_hotT, i, k)
                        done(pe, s_win, i, k, 16 * GT)
                        done(pe, s_used, i, k - 2)
                        bank, s = psum[2 + k % 2], k % 2
                        if layer == 1:
                            done(pe, s_xe, i, k, 16)
                        for j in range(GT):
                            hot = onehotT[s][:, j * P:(j + 1) * P]
                            if layer == 0:
                                last = nc.tensor.matmul(bank[:, j * D:(j + 1) * D], hot, window[s][:, j * D:(j + 1) * D], start=True, stop=True)
                            else:
                                w = window[s][:, j * H:(j + 1) * H]
                                nc.tensor.matmul(bank[:, j * H:(j + 1) * H], hot, w, start=True, stop=True)
                                o = bank[:, (GT + j) * H:(GT + j + 1) * H]
                                nc.tensor.matmul(o, hot, w, start=True, stop=False)
                                last = nc.tensor.matmul(o, xe[s][:, j * P:(j + 1) * P], w4, start=False, stop=True)
                        last.then_inc(s_side[s], 1)

                    transposes(0, 0)
                    def step_pe(i):
                        for k in range(4):
                            transposes(i, k + 1)
                            side(i, k)
                    loop(pe, G // 4, step_pe)

                @block.vector
                def _(dve):
                    if layer == 1:
                        nc.vector.memset(blockdiag, 0.0).then_inc(s_zero, 1)
                        dve.wait_ge(s_w4, 1)
                        nc.vector.tensor_copy(w4, psum[4][:, 0:H]).then_inc(s_w4, 1)

                    def one_hots(i, k):
                        done(dve, s_T, i, k - 2)
                        rel = cols(REL, (i * 4 + k) * GT, GT).unsqueeze(2).broadcast_to([P, GT, P])
                        nc.vector.tensor_tensor(onehot[k % 2].rearrange("p (t n) -> p t n", t=GT), rel,
                                                iota_row[:, :].unsqueeze(1).broadcast_to([P, GT, P]), ALU.is_equal).then_inc(s_hot[k % 2], 1)

                    def logits(i, k):
                        done(dve, s_side, i, k)
                        done(dve, s_got, i, k, 16 * GT)
                        done(dve, s_log, i, k - 2)
                        rows = got[k].rearrange("p (t d) -> p t d", t=GT)
                        at, bank, w = (i * 4 + k) * GT * H, psum[2 + k % 2], work[k % 2]
                        if layer == 0:
                            nc.vector.tensor_tensor(w.rearrange("p (t d) -> p t d", t=GT), rows[:, :, 0:D],
                                                    bank[:, :].rearrange("p (t d) -> p t d", t=GT), ALU.mult).then_inc(s_used[k], 1)
                            done(dve, s_used, i, k)
                            nc.vector.tensor_reduce(cols(W1, at, GT * H), w.rearrange("p (a d) -> p a d", d=HD), AX, ALU.add).then_inc(s_log[k % 2], 1)
                        else:
                            w1, w2 = w[:, 0:GT * H], w[:, GT * H:2 * GT * H]
                            nc.vector.tensor_copy(w2, bank[:, GT * H:2 * GT * H])
                            nc.vector.tensor_tensor(w1.rearrange("p (t h) -> p t h", t=GT), rows[:, :, D:D + H],
                                                    bank[:, 0:GT * H].rearrange("p (t h) -> p t h", t=GT), ALU.add).then_inc(s_used[k], 1)
                            done(dve, s_used, i, k)
                            nc.vector.scalar_tensor_tensor(cols(W1, at, GT * H), w1, SLOPE, w1, ALU.mult, ALU.max)
                            nc.vector.scalar_tensor_tensor(cols(W2, at, GT * H), w2, SLOPE, w2, ALU.mult, ALU.max).then_inc(s_log[k % 2], 1)

                    one_hots(0, 0)
                    def step_dve(i):
                        for k in range(4):
                            one_hots(i, k + 1)
                            logits(i, k)
                    loop(dve, G // 4, step_dve)

        def transpose_all(name, src, dst):
            stage = SCR[:, SCR.shape[1] - GT * P:]
            s_stage, s_T, s_copied = (sem(f"{name}_{x}") for x in ("stage", "T", "copied"))
            with nc.Block() as block:
                @block.scalar
                def _(act):
                    def step_act(i):
                        wait(act, s_T, i)
                        nc.scalar.copy(stage, cols(src, i * GT * P, GT * P)).then_inc(s_stage, 1)
                    loop(act, C // GT, step_act)

                @block.tensor
                def _(pe):
                    def step_pe(i):
                        wait(pe, s_stage, i + 1)
                        wait(pe, s_copied, i)
                        for j in range(GT):
                            last = nc.tensor.transpose(psum[0][:, j * P:(j + 1) * P], stage[:, j * P:(j + 1) * P], ident[:, :])
                        last.then_inc(s_T, 1)
                    loop(pe, C // GT, step_pe)

                @block.vector
                def _(dve):
                    def step_dve(i):
                        wait(dve, s_T, i + 1)
                        nc.vector.tensor_copy(cols(dst, i * GT * P, GT * P), psum[0][:, :]).then_inc(s_copied, 1)
                    loop(dve, C // GT, step_dve)

        def edge_softmax(name, W, scale):
            carve = Carve()
            keep_prev, keep_next, head_part, tail_part, cost = (carve(SL) for _ in range(5))
            flags, carry = carve(2), carve(2)
            strip_keep, strip_cost = carve(2 * P), carve(2 * P)
            strip_f, strip_b = carve(P + 1), carve(P + 1)
            rows = SUM[:, 0:ET * H]
            heads = rows.rearrange("p (h n) -> p h n", h=H)
            fwd, bwd, dst_f = (SUM[:, (H + n) * SL:(H + n + 1) * SL] for n in range(3))
            s_dma, s_idx, s_heads, s_chain, s_ends, s_Tends, s_strips, s_Tstrips, s_sub, s_exp, s_weights, s_back = (
                sem(f"{name}_{x}") for x in ("dma", "idx", "heads", "chain", "ends", "Tends", "strips", "Tstrips",
                                             "sub", "exp", "weights", "back"))
            rows3 = rows.rearrange("p (c e) -> p c e", e=P)
            rows_of = lambda table: table.rearrange("(c r) e -> r c e", r=P)
            heads_of = lambda table, h: table.rearrange("(p t h) e -> h p t e", h=H, t=ST)[h]

            transpose_all(f"{name}_out", W, rows)
            with nc.Block() as block:
                @block.sync
                def _(sp):
                    line = A["dst_line"]
                    for n, to in ((0, keep_prev), (1, cost), (2, keep_next)):
                        sp.dma_start(to.bitcast(I32), line[n:n + EP].rearrange("(p n) -> p n", p=P)).then_inc(s_idx, 16)
                    sp.dma_start(rows_of(rows_out), rows3).then_inc(s_dma, 16)
                    sp.wait_ge(s_dma, 16)
                    for h in range(H):
                        sp.dma_start(heads[:, h, :].rearrange("p (t e) -> p t e", e=P), heads_of(rows_out, h)).then_inc(s_heads, 16)
                    for h in range(H):
                        sp.wait_ge(s_weights, h + 1)
                        sp.dma_start(heads_of(rows_in, h), heads[:, h, :].rearrange("p (t e) -> p t e", e=P)).then_inc(s_dma, 16)
                    sp.wait_ge(s_dma, (1 + H) * 16)
                    sp.dma_start(rows3, rows_of(rows_in)).then_inc(s_back, 16)
                    sp.wait_ge(s_back, 16)

                @block.vector
                def _(dve):
                    link = chained(dve, s_chain)
                    v, turns = nc.vector, [0]
                    dve.wait_ge(s_idx, 3 * 16)
                    link(v.tensor_copy(cost, cost.bitcast(I32)))
                    link(v.tensor_copy(keep_prev, keep_prev.bitcast(I32)))
                    link(v.tensor_copy(keep_next, keep_next.bitcast(I32)))
                    dve.wait_ge(s_dma, 16)
                    link(v.tensor_copy(dst_f, cost))
                    link(v.tensor_tensor(keep_prev, keep_prev, dst_f, ALU.is_equal))
                    link(v.tensor_tensor(keep_next, keep_next, dst_f, ALU.is_equal))
                    link(v.tensor_scalar(head_part, dst_f, dst_f[:, 0:1], keep_prev[:, 0:1], ALU.is_equal, ALU.mult))
                    link(v.tensor_scalar(tail_part, dst_f, dst_f[:, SL - 1:SL], keep_next[:, SL - 1:SL], ALU.is_equal, ALU.mult))
                    link(v.tensor_reduce(flags[:, 0:1], keep_prev, AX, ALU.min))
                    v.tensor_reduce(flags[:, 1:2], keep_next, AX, ALU.min).then_inc(s_ends, 1)
                    turns[0] = 1
                    dve.wait_ge(s_Tends, 1)
                    link(v.tensor_copy(strip_keep[0:1, :], psum[0][0:1, 0:2 * P]))
                    link(v.tensor_scalar(strip_cost[0:1, :], strip_keep[0:1, :], 1.0, BIG, ALU.subtract, ALU.mult))
                    dve.wait_ge(s_heads, H * 16)

                    def carries(per_strip, none, op0, op1):
                        turns[0] += 1
                        dve.sem_inc(s_ends, 1)
                        dve.wait_ge(s_Tends, turns[0])
                        link(v.memset(strip_f[0:1, 0:1], none))
                        link(v.memset(strip_b[0:1, P:P + 1], none))
                        link(v.tensor_tensor_scan(strip_f[0:1, 1:P + 1], per_strip[0:1, 0:P], psum[0][0:1, 0:P], none, op0, op1))
                        v.tensor_tensor_scan(strip_b[0:1, 0:P][:, ::-1], per_strip[0:1, P:2 * P][:, ::-1],
                                             psum[0][0:1, P:2 * P][:, ::-1], none, op0, op1).then_inc(s_strips, 1)
                        dve.wait_ge(s_Tstrips, turns[0] - 1)
                        link(v.tensor_copy(carry, psum[1][:, 0:2]))

                    for h in range(H):
                        a = heads[:, h, :]
                        link(v.tensor_scalar(cost, keep_prev, 1.0, BIG, ALU.subtract, ALU.mult))
                        link(v.tensor_tensor_scan(fwd, cost, a, -BIG, ALU.add, ALU.max))
                        link(v.tensor_scalar(cost, keep_next, 1.0, BIG, ALU.subtract, ALU.mult))
                        link(v.tensor_tensor_scan(bwd[:, ::-1], cost[:, ::-1], a[:, ::-1], -BIG, ALU.add, ALU.max))
                        carries(strip_cost, -BIG, ALU.add, ALU.max)
                        link(v.tensor_scalar(cost, head_part, 1.0, BIG, ALU.subtract, ALU.mult))
                        link(v.scalar_tensor_tensor(fwd, cost, carry[:, 0:1], fwd, ALU.add, ALU.max))
                        link(v.tensor_scalar(cost, tail_part, 1.0, BIG, ALU.subtract, ALU.mult))
                        link(v.scalar_tensor_tensor(bwd, cost, carry[:, 1:2], bwd, ALU.add, ALU.max))
                        link(v.tensor_tensor(fwd, fwd, bwd, ALU.max))
                        v.tensor_tensor(a, a, fwd, ALU.subtract).then_inc(s_sub, 1)
                        dve.wait_ge(s_exp, h + 1)
                        link(v.tensor_tensor_scan(fwd, keep_prev, a, 0.0, ALU.mult, ALU.add))
                        link(v.tensor_tensor_scan(bwd[:, ::-1], keep_next[:, ::-1], a[:, ::-1], 0.0, ALU.mult, ALU.add))
                        carries(strip_keep, 0.0, ALU.mult, ALU.add)
                        link(v.scalar_tensor_tensor(fwd, head_part, carry[:, 0:1], fwd, ALU.mult, ALU.add))
                        link(v.scalar_tensor_tensor(bwd, tail_part, carry[:, 1:2], bwd, ALU.mult, ALU.add))
                        link(v.tensor_tensor(bwd, bwd, a, ALU.subtract))
                        link(v.tensor_tensor(fwd, fwd, bwd, ALU.add))
                        link(v.reciprocal(fwd, fwd))
                        v.tensor_tensor(a, a, fwd, ALU.mult).then_inc(s_weights, 1)
                        dve.wait_ge(s_weights, h + 1)

                @block.scalar
                def _(act):
                    for h in range(H):
                        act.wait_ge(s_sub, h + 1)
                        nc.scalar.activation(heads[:, h, :], heads[:, h, :], ACT.Exp, scale=scale).then_inc(s_exp, 1)

                @block.tensor
                def _(pe):
                    for n in range(1 + 2 * H):
                        ends = (flags[:, 0:1], flags[:, 1:2]) if n == 0 else (fwd[:, SL - 1:SL], bwd[:, 0:1])
                        pe.wait_ge(s_ends, n + 1)
                        nc.tensor.transpose(psum[0][0:1, 0:P], ends[0], ident[:, :])
                        nc.tensor.transpose(psum[0][0:1, P:2 * P], ends[1], ident[:, :]).then_inc(s_Tends, 1)
                        if n:
                            pe.wait_ge(s_strips, n)
                            nc.tensor.transpose(psum[1][:, 0:1], strip_f[0:1, 0:P], ident[0:1, 0:1])
                            nc.tensor.transpose(psum[1][:, 1:2], strip_b[0:1, 1:P + 1], ident[0:1, 0:1]).then_inc(s_Tstrips, 1)
            transpose_all(f"{name}_in", rows, W)

        def pass_b(layer):
            name = f"b{layer}"
            carve = Carve()
            kept = [carve(GT * D) for _ in range(4)]
            onehot, msg = ([carve(GT * P) for _ in range(2)] for _ in range(2))
            if layer == 1:
                xe, total = ([carve(GT * P) for _ in range(2)] for _ in range(2))
                w_edge_T = carve(D)
            first = carve(ET)[0:1, :].bitcast(I32)
            s_first = sem(f"{name}_first")
            s_kept = sems(f"{name}_kept", 4)
            s_msg = sems(f"{name}_msg", 4)
            s_hot, s_sum, s_free = (sems(f"{name}_{x}", 2) for x in ("onehot", "sum", "free"))
            s_add, s_zero = sem(f"{name}_add"), sem(f"{name}_zero")
            if layer == 1:
                s_xe, s_he, s_me, s_total = (sems(f"{name}_{x}", 2) for x in ("xedge", "hedge", "msgedge", "total"))
            s_read = s_sum if layer == 0 else s_total
            full = msg if layer == 0 else total
            with nc.Block() as block:
                @block.sync
                def _(sp):
                    sp.dma_start(first, A["tile_first"]).then_inc(s_first, 16)
                    if layer == 1:
                        sp.dma_start(w_edge_T, A["W_edge_T"]).then_inc(s_first, 16)
                    def step_sp(i):
                        for k in range(4):
                            g = i * 4 + k
                            done(sp, s_msg, i, k - 4)
                            sp.dma_start(kept[k], gathered[bass.ds(g, 1), :, :].rearrange("a p n -> (a p) n")).then_inc(s_kept[k], 16)
                            if layer == 1:
                                done(sp, s_he, i, k - 2)
                                sp.dma_start(xe[k % 2], A["xe_T"][:, bass.ds(g * GT * P, GT * P)]).then_inc(s_xe[k % 2], 16)
                    loop(sp, G // 4, step_sp)

                by_head = lambda t: t.rearrange("p (a d) -> p a d", d=HD)

                def weights_of(t, i, k):
                    return cols(t, (i * 4 + k) * GT * H, GT * H).unsqueeze(2).broadcast_to([P, GT * H, HD])

                @block.gpsimd
                def _(pool):
                    def step_pool(i):
                        for k in range(4):
                            done(pool, s_kept, i, k, 16)
                            done(pool, s_read, i, k - 2)
                            nc.gpsimd.tensor_tensor(by_head(msg[k % 2]), by_head(kept[k]), weights_of(W1, i, k), ALU.mult).then_inc(s_msg[k], 1)
                    loop(pool, G // 4, step_pool)

                @block.tensor
                def _(pe):
                    def edges(i, k):
                        done(pe, s_xe, i, k, 16)
                        done(pe, s_me, i, k - 2)
                        for j in range(GT):
                            last = nc.tensor.matmul(psum[4 + k % 2][:, j * D:(j + 1) * D], xe[k % 2][:, j * P:(j + 1) * P], w_edge_T, start=True, stop=True)
                        last.then_inc(s_he[k % 2], 1)

                    if layer == 1:
                        pe.wait_ge(s_first, 32)
                    def step_pe(i):
                        for k in range(4):
                            if layer == 1:
                                edges(i, k)
                            done(pe, s_hot, i, k)
                            done(pe, s_msg if layer == 0 else s_total, i, k)
                            done(pe, s_free, i, k - 2)
                            for j in range(GT):
                                last = nc.tensor.matmul(psum[k % 2][:, j * P:(j + 1) * P], full[k % 2][:, j * D:(j + 1) * D],
                                                        onehot[k % 2][:, j * P:(j + 1) * P], start=True, stop=True)
                            last.then_inc(s_sum[k % 2], 1)
                    loop(pe, G // 4, step_pe)

                @block.vector
                def _(dve):
                    nc.vector.memset(SUM[:, :], 0.0).then_inc(s_zero, 1)
                    dve.wait_ge(s_zero, 1)
                    dve.wait_ge(s_first, 32 if layer == 1 else 16)

                    def one_hots(i, k):
                        done(dve, s_sum, i, k - 2)
                        rel = cols(REL, (i * 4 + k) * GT, GT).unsqueeze(2).broadcast_to([P, GT, P])
                        nc.vector.tensor_tensor(onehot[k % 2].rearrange("p (t n) -> p t n", t=GT), rel,
                                                iota_row[:, :].unsqueeze(1).broadcast_to([P, GT, P]), ALU.is_equal).then_inc(s_hot[k % 2], 1)

                    def edge_messages(i, k):
                        done(dve, s_he, i, k)
                        done(dve, s_sum, i, k - 2)
                        nc.vector.tensor_tensor(by_head(total[k % 2]), by_head(psum[4 + k % 2][:, :]), weights_of(W2, i, k), ALU.mult).then_inc(s_me[k % 2], 1)
                        done(dve, s_msg, i, k)
                        done(dve, s_me, i, k)
                        nc.vector.tensor_tensor(total[k % 2], total[k % 2], msg[k % 2], ALU.add).then_inc(s_total[k % 2], 1)

                    def add(i, k, starts):
                        done(dve, s_sum, i, k)
                        for j in range(GT):
                            t = (i * 4 + k) * GT + j
                            wait(dve, s_add, t)
                            w = SUM[:, bass.ds(starts[k * GT + j], P)]
                            last = nc.vector.tensor_tensor(w, w, psum[k % 2][:, j * P:(j + 1) * P], ALU.add).then_inc(s_add, 1)
                        dve.wait_ge(s_add, (i * 4 + k + 1) * GT)
                        dve.sem_inc(s_free[k % 2], 1)

                    def step_dve(i):
                        starts = window_starts(dve, mybir.EngineType.DVE, first, i)
                        for k in range(4):
                            one_hots(i, k)
                            if layer == 1:
                                edge_messages(i, k)
                            add(i, k, starts)
                    loop(dve, G // 4, step_dve)

        def sums_to_rows(name, onto_x):
            carve = Carve()
            stage = [carve(P) for _ in range(2)]
            s_stage, s_T, s_copied = (sems(f"{name}_{x}", 2) for x in ("stage", "T", "copied"))
            with nc.Block() as block:
                @block.scalar
                def _(act):
                    def step_act(i):
                        for s in range(2):
                            wait(act, s_T[s], i)
                            nc.scalar.copy(stage[s], cols(SUM, (i * 2 + s) * P, P)).then_inc(s_stage[s], 1)
                    loop(act, NT // 2, step_act)

                @block.tensor
                def _(pe):
                    def step_pe(i):
                        for s in range(2):
                            wait(pe, s_stage[s], i + 1)
                            wait(pe, s_copied[s], i)
                            nc.tensor.transpose(psum[s][:, 0:P], stage[s], ident[:, :]).then_inc(s_T[s], 1)
                    loop(pe, NT // 2, step_pe)

                @block.vector
                def _(dve):
                    def step_dve(i):
                        for s in range(2):
                            wait(dve, s_T[s], i + 1)
                            if onto_x:
                                x = X[:, bass.ds(i * 2 + s, 1), :].rearrange("p a d -> p (a d)")
                                nc.vector.tensor_tensor(x, x, psum[s][:, 0:P], ALU.add).then_inc(s_copied[s], 1)
                            else:
                                nc.vector.tensor_copy(cols(SUM, (i * 2 + s) * P, P), psum[s][:, 0:P]).then_inc(s_copied[s], 1)
                    loop(dve, NT // 2, step_dve)

        def gate_and_norm():
            chunk_tiles = max(n for n in range(1, NT + 1) if NT % n == 0 and n * D <= SCR.shape[1] // 2)
            carve = Carve()
            tmp = carve(chunk_tiles * D)
            wg, gamma, beta = carve(3 * D), carve(D), carve(D)
            z, dev, var, mean = carve(NT), carve(NT), carve(NT), carve(NT)
            stats = carve(6 * NT)
            alpha, neg_bg = carve(1), carve(1)
            skip = W[:, 0:NP]
            s_load, s_chain, s_z, s_e, s_stats, s_var, s_std = (sem(f"g_{x}") for x in ("load", "chain", "z", "e", "stats", "var", "std"))
            t3 = lambda t: t.rearrange("p (t d) -> p t d", d=D)
            with nc.Block() as block:
                @block.sync
                def _(sp):
                    sp.dma_start(t3(skip), skip_table.rearrange("(t p) d -> p t d", p=P)).then_inc(s_load, 16)
                    for to, of in ((wg, A["Wg"].rearrange("n a -> (n a)")), (gamma, A["gamma"]), (beta, A["beta"]), (alpha, A["alpha"]), (neg_bg, A["bg"])):
                        sp.dma_start(to, of.partition_broadcast(P)).then_inc(s_load, 16)
                    sp.wait_ge(s_load, 6 * 16)

                @block.scalar
                def _(act):
                    act.wait_ge(s_z, 1)
                    nc.scalar.activation(z, z, ACT.Exp, scale=-1.0).then_inc(s_e, 1)
                    act.wait_ge(s_var, 1)
                    nc.scalar.activation(var, var, ACT.Sqrt).then_inc(s_std, 1)

                @block.vector
                def _(dve):
                    link, v = chained(dve, s_chain), nc.vector
                    over = lambda row, n: row.unsqueeze(1).broadcast_to([P, n, D])
                    spread = lambda col, n: col.unsqueeze(2).broadcast_to([P, n, D])
                    dve.wait_ge(s_load, 6 * 16)
                    for c in range(NT // chunk_tiles):
                        n = chunk_tiles
                        sl, ts = slice(c * n * D, (c + 1) * n * D), slice(c * n, (c + 1) * n)
                        sk, agg = skip[:, sl], SUM[:, sl]
                        link(v.tensor_tensor(t3(tmp), t3(sk), over(wg[:, 0:D], n), ALU.mult))
                        link(v.tensor_reduce(z[:, ts], t3(tmp), AX, ALU.add))
                        link(v.tensor_tensor(t3(tmp), t3(agg), over(wg[:, D:2 * D], n), ALU.mult))
                        link(v.tensor_reduce(var[:, ts], t3(tmp), AX, ALU.add))
                        link(v.tensor_tensor(sk, sk, agg, ALU.subtract))
                        link(v.tensor_tensor(t3(tmp), t3(sk), over(wg[:, 2 * D:3 * D], n), ALU.mult))
                        link(v.tensor_reduce(dev[:, ts], t3(tmp), AX, ALU.add))
                    link(v.tensor_tensor(z, z, var, ALU.add))
                    link(v.scalar_tensor_tensor(z, z, neg_bg, dev, ALU.add, ALU.add))
                    dve.sem_inc(s_z, 1)
                    dve.wait_ge(s_e, 1)
                    link(v.tensor_scalar(z, z, 1.0, None, ALU.add))
                    link(v.reciprocal(z, z))
                    link(v.tensor_tensor(t3(skip), t3(skip), spread(z, NT), ALU.mult))
                    link(v.tensor_tensor(SUM[:, :], SUM[:, :], skip, ALU.add))
                    st = stats.rearrange("p (t k) -> p t k", k=6)
                    for t in range(NT):
                        v.bn_stats(stats[:, 6 * t:6 * t + 6], SUM[:, t * D:(t + 1) * D]).then_inc(s_stats, 1)
                    dve.wait_ge(s_stats, NT)
                    moments(link, st, mean, dev, var, s_var)
                    dve.wait_ge(s_std, 1)
                    link(v.reciprocal(var, var))
                    link(v.tensor_tensor(t3(SUM[:, :]), t3(SUM[:, :]), spread(mean, NT), ALU.subtract))
                    link(v.tensor_tensor(t3(SUM[:, :]), t3(SUM[:, :]), spread(var, NT), ALU.mult))
                    link(v.tensor_tensor(t3(SUM[:, :]), t3(SUM[:, :]), over(gamma, NT), ALU.mult))
                    link(v.tensor_tensor(t3(SUM[:, :]), t3(SUM[:, :]), over(beta, NT), ALU.add))
                    link(v.tensor_scalar(skip, SUM[:, :], 0.0, alpha, ALU.min, ALU.mult))
                    link(v.scalar_tensor_tensor(SUM[:, :], SUM[:, :], 0.0, skip, ALU.max, ALU.add))
                    flat = X[:, :, :].rearrange("p t d -> p (t d)")
                    link(v.tensor_tensor(flat, flat, SUM[:, :], ALU.add))

        def store():
            s_stored = sem("o_stored")
            whole, rest = n_nodes // P, n_nodes % P
            with nc.Block() as block:
                @block.sync
                def _(sp):
                    sp.dma_start(A["out"][0:whole * P, :].rearrange("(t p) d -> p t d", p=P), X[:, 0:whole, :]).then_inc(s_stored, 16)
                    if rest:
                        sp.dma_start(A["out"][whole * P:n_nodes, :], X[0:rest, whole, :]).then_inc(s_stored, 16)
                    sp.wait_ge(s_stored, 16 * (2 if rest else 1))

        phase(setup)
        phase(node_tables, 0)
        phase(pass_a, 0)
        phase(edge_softmax, "s0", W1, float(HD) ** -0.5)
        phase(pass_b, 0)
        phase(sums_to_rows, "r0", False)
        phase(gate_and_norm)
        phase(node_tables, 1)
        phase(pass_a, 1)
        phase(edge_softmax, "s1", W1, 1.0)
        phase(edge_softmax, "s2", W2, 1.0)
        phase(pass_b, 1)
        phase(sums_to_rows, "r1", True)
        phase(store)


def kernel(x, src, dst, edge_attr_128, L0_gnn_Wq, L0_gnn_bq, L0_gnn_Wk, L0_gnn_bk, L0_gnn_Wv, L0_gnn_bv,
           L0_gnn_Ws, L0_gnn_bs, L0_gnn_Wg, L0_gnn_bg, L0_gnn_gamma, L0_gnn_beta, L0_gnn_alpha,
           L1_gnn_W_src, L1_gnn_W_dst, L1_gnn_W_edge, L1_gnn_attn_src, L1_gnn_attn_dst, L1_gnn_attn_edge):
    import concourse.bacc as bacc
    from concourse.bass_utils import run_bass_kernel_spmd

    n_nodes, n_edges = x.shape[0], src.shape[0]
    NT, ET = sizes(n_nodes, n_edges)
    ep = ET * P
    f = lambda a: np.asarray(a)
    x_pad = np.zeros((NT * P, D), np.float32)
    x_pad[:n_nodes] = f(x)
    src_pad = np.zeros(ep, np.int32)
    src_pad[:n_edges] = f(src)
    dst_line = np.full(ep + 2, -1, np.int32)
    dst_line[1:n_edges + 1] = f(dst)
    dst_line[n_edges + 1:ep + 1] = n_nodes
    dst_pad = dst_line[1:-1]
    xe_T = np.zeros((D, ep), np.float32)
    xe_T[:, :n_edges] = f(edge_attr_128).T
    arrays = {
        "x": x_pad, "xe_T": xe_T, "dst_line": dst_line,
        "src_tiles": src_pad.reshape(ET, P).T, "dst_tiles": dst_pad.reshape(ET, P).T,
        "tile_first": dst_pad.reshape(ET, P)[:, 0].reshape(1, ET),
        "Wq": f(L0_gnn_Wq), "Wk": f(L0_gnn_Wk), "Wv": f(L0_gnn_Wv), "Ws": f(L0_gnn_Ws),
        "bq": f(L0_gnn_bq), "bk": f(L0_gnn_bk), "bv": f(L0_gnn_bv), "bs": f(L0_gnn_bs),
        "Wg": f(L0_gnn_Wg), "bg": f(L0_gnn_bg), "gamma": f(L0_gnn_gamma), "beta": f(L0_gnn_beta),
        "alpha": f(L0_gnn_alpha).reshape(1),
        "W_src_T": f(L1_gnn_W_src).T, "W_dst_T": f(L1_gnn_W_dst).T, "W_edge": f(L1_gnn_W_edge), "W_edge_T": f(L1_gnn_W_edge).T,
        "attn_src": f(L1_gnn_attn_src), "attn_dst": f(L1_gnn_attn_dst), "attn_edge": f(L1_gnn_attn_edge),
    }
    nc = bacc.Bacc("TRN2", target_bir_lowering=False, num_devices=1)
    ins, A = {}, {}
    for name, a in arrays.items():
        a = np.ascontiguousarray(a)
        ins[f"in_{name}"] = a
        A[name] = nc.dram_tensor(f"in_{name}", a.shape, mybir.dt.from_np(a.dtype), kind="ExternalInput").ap()
    A["out"] = nc.dram_tensor("out", (n_nodes, D), F32, kind="ExternalOutput").ap()
    build(nc, A, n_nodes, n_edges)
    r = run_bass_kernel_spmd(nc, [ins], core_ids=[0])
    return r.results[0]["out"]
```

```python
from contextlib import ExitStack

import numpy as np

import concourse.bass as bass
from concourse import mybir
from concourse.alu_op_type import AluOpType as ALU

ACT = mybir.ActivationFunctionType
AX = mybir.AxisListType.X
F32 = mybir.dt.float32
I32 = mybir.dt.int32
BF16 = mybir.dt.bfloat16

P = 128
D = 128
H = 4
HD = D // H
GT = 4
CT = P // H
EPS = 1e-5
SLOPE = 0.2
BIG = 1e30


def sizes(n_nodes, n_edges):
    node_tiles = -(-(n_nodes + P + 1) // P)
    node_tiles += node_tiles % 2
    unit = P * P
    return node_tiles, -(-n_edges // unit) * P


def build(nc, A, n_nodes, n_edges):
    NT, ET = sizes(n_nodes, n_edges)
    NP = NT * P
    EP = ET * P
    G = ET // GT
    C = ET // CT
    ST = ET // P
    SL = ST * P
    assert G % 4 == 0 and G >= 12 and ET * H == C * P and C % GT == 0 and NP <= 2 * ET * H and 7 * SL <= NP

    def dram(name, shape, dt=F32):
        return nc.dram_tensor(name, shape, dt, kind="Internal").ap()

    qv_table = dram("qv_table", (NP, 2 * D))
    k_table = dram("k_table", (NP, D))
    skip_table = dram("skip_table", (NP, D))
    hs_table = dram("hs_table", (NP, D + H))
    ed_table = dram("ed_table", (NP, 3 * H), BF16)
    gathered = dram("gathered", (G, P, GT * D))
    rows_out = dram("rows_out", (ET * H, P))
    rows_in = dram("rows_in", (ET * H, P))

    with ExitStack() as ctx:
        def sb(name, shape, dt=F32):
            return ctx.enter_context(nc.sbuf_tensor(name, shape, dt))

        phase_sems = []

        def sem(name):
            phase_sems.append(nc.alloc_semaphore(name=name))
            return phase_sems[-1]

        def phase(program, *args):
            program(*args)
            nc.clear_and_free_semaphores(phase_sems)
            nc.all_engine_barrier()
            phase_sems.clear()

        def sems(name, n):
            return [sem(f"{name}{i}") for i in range(n)]

        X = sb("X", [P, NT, D])
        SUM = sb("SUM", [P, NP])
        W = sb("W", [P, 2 * ET * H])
        W1, W2 = W[:, 0:ET * H], W[:, ET * H:2 * ET * H]
        REL = sb("REL", [P, ET])
        SRC = sb("SRC", [P, ET], I32)
        SCR = sb("SCR", [P, 9472])
        ident = sb("ident", [P, P])
        ident_b = sb("ident_b", [P, P], BF16)
        iota_row = sb("iota_row", [P, P])
        psum = [ctx.enter_context(nc.psum_tensor(f"bank{i}", [P, 512], F32)) for i in range(8)]

        class Carve:
            def __init__(self):
                self.at = 0

            def __call__(self, n):
                self.at += n
                assert self.at <= SCR.shape[1], self.at
                return SCR[:, self.at - n:self.at]

        def chained(eng, s):
            count = [0]

            def link(ins):
                count[0] += 1
                ins.then_inc(s, 1)
                eng.wait_ge(s, count[0])
            return link

        def wait(eng, s, value):
            if not isinstance(value, int) or value > 0:
                eng.wait_ge(s, value)

        def done(eng, s, i, k, each=1, less=0):
            n = len(s)
            wait(eng, s[k % n], (i * (4 // n) + k // n + 1) * each - less)

        def loop(eng, n, body):
            body(0)
            if n > 1:
                with eng.Fori(1, n) as i:
                    body(i)

        def loop_ahead(eng, n, body):
            body(0, False)
            with eng.Fori(1, n - 1) as i:
                body(i, False)
            body(n - 1, True)

        def window_starts(eng, engine, first, i):
            return nc.values_load_multi_w_load_instructions(first[0:1, bass.ds(i * 4 * GT, 4 * GT)], engines=[engine],
                                                            min_val=0, max_val=n_nodes,
                                                            skip_runtime_bounds_check_because="every dst is a node, or the padding's row")[1]

        def cols(t, start, n):
            return t[:, bass.ds(start, n)]

        def setup():
            s_load, s_const, s_iota, s_first = sem("set_load"), sem("set_const"), sem("set_iota"), sem("set_first")
            s_chain = sem("set_chain")
            dst_i = SUM[:, 0:ET].bitcast(I32)
            first_i = SUM[:, ET:2 * ET].bitcast(I32)
            iota_i = SUM[:, 2 * ET:2 * ET + P].bitcast(I32)
            with nc.Block() as block:
                @block.sync
                def _(sp):
                    sp.dma_start(SRC[:, :], A["src_tiles"]).then_inc(s_load, 16)
                    sp.dma_start(dst_i, A["dst_tiles"]).then_inc(s_load, 16)
                    sp.dma_start(first_i, A["tile_first"].partition_broadcast(P)).then_inc(s_load, 16)
                    for c in range(2):
                        ts = slice(c * NT // 2, (c + 1) * NT // 2)
                        sp.dma_start(X[:, ts, :], A["x"].rearrange("(t p) d -> p t d", p=P)[:, ts, :]).then_inc(s_load, 16)
                    sp.wait_ge(s_load, 5 * 16)

                @block.gpsimd
                def _(pool):
                    pool.memset(ident[:, :], 0.0).then_inc(s_const, 1)
                    pool.iota(iota_i, pattern=[[1, P]], base=0, channel_multiplier=0).then_inc(s_iota, 1)
                    pool.wait_ge(s_const, 1)
                    pool.affine_select(out=ident[:, :], in_=ident[:, :], compare_op=ALU.not_equal, fill=1.0,
                                       base=0, pattern=[[-1, P]], channel_multiplier=1).then_inc(s_const, 1)

                @block.vector
                def _(dve):
                    link = chained(dve, s_chain)
                    dve.wait_ge(s_iota, 1)
                    link(nc.vector.tensor_copy(iota_row[:, :], iota_i))
                    dve.wait_ge(s_const, 2)
                    link(nc.vector.tensor_copy(ident_b[:, :], ident[:, :]))
                    dve.wait_ge(s_load, 5 * 16)
                    link(nc.vector.tensor_tensor(REL[:, :], dst_i, first_i, ALU.subtract))

        def moments(link, st, mean, dev, var, s_var):
            link(nc.vector.tensor_tensor(mean, st[:, :, 1], st[:, :, 4], ALU.add))
            link(nc.vector.tensor_scalar(mean, mean, 0.5, None, ALU.mult))
            link(nc.vector.tensor_tensor(dev, st[:, :, 1], st[:, :, 4], ALU.subtract))
            link(nc.vector.tensor_scalar(dev, dev, 0.5, None, ALU.mult))
            link(nc.vector.tensor_tensor(dev, dev, dev, ALU.mult))
            link(nc.vector.tensor_tensor(var, st[:, :, 2], st[:, :, 5], ALU.add))
            link(nc.vector.tensor_scalar(var, var, 1.0 / D, EPS, ALU.mult, ALU.add))
            nc.vector.tensor_tensor(var, var, dev, ALU.add).then_inc(s_var, 1)

        def norm_stats(name, stats, scale_out, shift_out, tmp):
            s_stats, s_chain, s_var, s_std = (sem(f"{name}_{x}") for x in ("stats", "chain", "var", "std"))
            st = stats.rearrange("p (t k) -> p t k", k=6)
            with nc.Block() as block:
                @block.vector
                def _(dve):
                    link = chained(dve, s_chain)
                    def step_dve(i):
                        for k in range(2):
                            t = bass.ds(i * 2 + k, 1)
                            nc.vector.bn_stats(st[:, t, :].rearrange("p a k -> p (a k)"),
                                               X[:, t, :].rearrange("p a d -> p (a d)")).then_inc(s_stats, 1)
                    loop(dve, NT // 2, step_dve)
                    dve.wait_ge(s_stats, NT)
                    mean, dev, var = tmp[:, 0:NT], tmp[:, NT:2 * NT], tmp[:, 2 * NT:3 * NT]
                    moments(link, st, mean, dev, var, s_var)
                    dve.wait_ge(s_std, 1)
                    link(nc.vector.reciprocal(scale_out, var))
                    link(nc.vector.scalar_tensor_tensor(shift_out, mean, -1.0, scale_out, ALU.mult, ALU.mult))

                @block.scalar
                def _(act):
                    act.wait_ge(s_var, 1)
                    var = tmp[:, 2 * NT:3 * NT]
                    nc.scalar.activation(var, var, ACT.Sqrt).then_inc(s_std, 1)


        def node_tables(layer):
            name = f"t{layer}"
            width = 4 * D if layer == 0 else 2 * D
            carve = Carve()
            stats, tmp = carve(6 * NT), carve(3 * NT)
            scale, shift = carve(NT), carve(NT)
            weights, extra = carve(width), carve(width)
            h, hT = ([carve(D) for _ in range(2)] for _ in range(2))
            out = [carve(4 * D if layer == 0 else D + H) for _ in range(2)]
            prod = carve(2 * D)
            norm_stats(f"n{layer}", stats, scale, shift, tmp)
            s_w = sem(f"{name}_weights")
            s_h, s_T, s_hT, s_mm, s_out, s_stored, s_free = (
                sems(f"{name}_{x}", 2) for x in ("h", "T", "hT", "mm", "out", "stored", "free"))
            s_prod = sem(f"{name}_prod")
            if layer == 0:
                loads = [(weights[:, n * D:(n + 1) * D], A[w]) for n, w in enumerate(("Wq", "Wv", "Wk", "Ws"))]
                loads += [(extra[:, n * D:(n + 1) * D], A[b].partition_broadcast(P)) for n, b in enumerate(("bq", "bv", "bk", "bs"))]
                stores = lambda rows, o: [(qv_table[rows, :], o[:, 0:2 * D]), (k_table[rows, :], o[:, 2 * D:3 * D]),
                                          (skip_table[rows, :], o[:, 3 * D:4 * D])]
            else:
                loads = [(weights[:, n * D:(n + 1) * D], A[w]) for n, w in enumerate(("W_src_T", "W_dst_T"))]
                loads += [(extra[:, n * D:(n + 1) * D], A[b].rearrange("h d -> (h d)").partition_broadcast(P)) for n, b in enumerate(("attn_src", "attn_dst"))]
                stores = lambda rows, o: [(hs_table[rows, :], o[:, 0:D + H])]
                e_dst, split = carve(NT * H), carve(NT * H * 3 // 2)
                parts = split.bitcast(BF16).rearrange("p (t q h) -> p t q h", q=3, h=H)
                s_split, s_parts = sem(f"{name}_split"), sem(f"{name}_parts")
            each = 16 * (3 if layer == 0 else 1)
            with nc.Block() as block:
                @block.sync
                def _(sp):
                    for to, of in loads:
                        sp.dma_start(to, of).then_inc(s_w, 16)
                    def step_sp(i):
                        for s in range(2):
                            wait(sp, s_out[s], i + 1)
                            for to, of in stores(bass.ds((i * 2 + s) * P, P), out[s]):
                                sp.dma_start(to, of).then_inc(s_stored[s], 16)
                    loop(sp, NT // 2, step_sp)
                    for s in range(2):
                        sp.wait_ge(s_stored[s], NT // 2 * each)
                    if layer == 1:
                        sp.wait_ge(s_split, 5)
                        sp.dma_start(ed_table.rearrange("(t p) n -> p t n", p=P), parts.rearrange("p t q h -> p t (q h)")).then_inc(s_parts, 16)
                        sp.wait_ge(s_parts, 16)

                @block.scalar
                def _(act):
                    def step_act(i):
                        for s in range(2):
                            t = i * 2 + s
                            wait(act, s_T[s], i)
                            nc.scalar.activation(h[s], X[:, bass.ds(t, 1), :].rearrange("p a d -> p (a d)"),
                                                 ACT.Relu, bias=cols(shift, t, 1), scale=cols(scale, t, 1)).then_inc(s_h[s], 1)
                        for s in range(2):
                            wait(act, s_T[s], i + 1)
                            wait(act, s_mm[s], i)
                            nc.scalar.copy(hT[s], psum[s][:, 0:D]).then_inc(s_hT[s], 1)
                    loop(act, NT // 2, step_act)

                @block.tensor
                def _(pe):
                    pe.wait_ge(s_w, len(loads) * 16)
                    def step_pe(i):
                        for s in range(2):
                            wait(pe, s_h[s], i + 1)
                            wait(pe, s_hT[s], i)
                            nc.tensor.transpose(psum[s][:, 0:D], h[s], ident[:, :]).then_inc(s_T[s], 1)
                        for s in range(2):
                            wait(pe, s_hT[s], i + 1)
                            wait(pe, s_free[s], i)
                            nc.tensor.matmul(psum[2 + s][:, 0:width], hT[s], weights, start=True, stop=True).then_inc(s_mm[s], 1)
                    loop(pe, NT // 2, step_pe)

                @block.vector
                def _(dve):
                    dve.wait_ge(s_w, len(loads) * 16)
                    def step_dve(i):
                        for s in range(2):
                            bank, o = psum[2 + s], out[s]
                            wait(dve, s_mm[s], i + 1)
                            wait(dve, s_stored[s], i * each)
                            if layer == 0:
                                nc.vector.tensor_tensor(o, bank[:, :], extra, ALU.add).then_inc(s_out[s], 1)
                                wait(dve, s_out[s], i + 1)
                                dve.sem_inc(s_free[s], 1)
                            else:
                                at = X[:, bass.ds(i * 2 + s, 1), :].rearrange("p a d -> p (a d)")
                                nc.vector.tensor_copy(o[:, 0:D], bank[:, 0:D])
                                nc.vector.tensor_tensor(at, at, bank[:, D:2 * D], ALU.add)
                                wait(dve, s_out[1 - s], i + s)
                                nc.vector.tensor_tensor(prod, bank[:, 0:2 * D], extra, ALU.mult).then_inc(s_free[s], 1)
                                wait(dve, s_free[s], i + 1)
                                by_head = prod.rearrange("p (a d) -> p a d", d=HD)
                                nc.vector.tensor_reduce(cols(e_dst, (i * 2 + s) * H, H), by_head[:, H:2 * H, :], AX, ALU.add)
                                nc.vector.tensor_reduce(o[:, D:D + H], by_head[:, 0:H, :], AX, ALU.add).then_inc(s_out[s], 1)
                    loop(dve, NT // 2, step_dve)
                    if layer == 1:
                        dve.wait_ge(s_out[1], NT // 2)
                        left = e_dst.rearrange("p (t h) -> p t h", h=H)
                        for q in range(3):
                            nc.vector.tensor_copy(parts[:, :, q, :], left).then_inc(s_split, 1)
                            if q < 2:
                                dve.wait_ge(s_split, 2 * q + 1)
                                nc.vector.tensor_tensor(left, left, parts[:, :, q, :], ALU.subtract).then_inc(s_split, 1)
                                dve.wait_ge(s_split, 2 * q + 2)

        def pass_a(layer):
            name = f"a{layer}"
            row = 2 * D if layer == 0 else D + H
            feat = D if layer == 0 else 0
            win = D if layer == 0 else 3 * H
            hot_dt, eye = (F32, ident) if layer == 0 else (BF16, ident_b)
            table = qv_table if layer == 0 else hs_table
            wtable = k_table if layer == 0 else ed_table
            carve = Carve()
            got = [carve(GT * row) for _ in range(4)]
            def carve_hot(n):
                return carve(n) if layer == 0 else carve(n // 2).bitcast(BF16)

            window = [carve_hot(GT * win) for _ in range(4)]
            onehot, onehotT = ([carve_hot(GT * P) for _ in range(2)] for _ in range(2))
            turned = [psum[s][:, :] if layer == 0 else psum[s][:, 0:GT * P // 2].bitcast(BF16) for s in range(2)]
            work = [carve(GT * D if layer == 0 else 3 * GT * H) for _ in range(2)]
            index = [carve(GT).bitcast(I32) for _ in range(4)]
            xe = [carve(GT * P) for _ in range(4)] if layer == 1 else None
            if layer == 1:
                w_edge, blockdiag, w4 = carve(D), carve(H), carve(H)
            turn = carve(2)[0:1, :]
            first = SUM[0:1, 0:ET].bitcast(I32)
            s_first, s_prep, s_w4, s_zero, s_turn = (sem(f"{name}_{x}") for x in ("first", "prep", "w4", "zero", "turn"))
            s_index, s_got, s_kept, s_used = (sems(f"{name}_{x}", 4) for x in ("index", "got", "kept", "used"))
            s_win, s_side = (sems(f"{name}_{x}", 4) for x in ("window", "side"))
            s_hot, s_T, s_hotT, s_log = (sems(f"{name}_{x}", 2) for x in ("onehot", "T", "onehotT", "logits"))
            if layer == 1:
                s_xe, s_part = sems(f"{name}_xedge", 4), sems(f"{name}_part", 2)

            with nc.Block() as block:
                @block.sync
                def _(sp):
                    sp.dma_start(first, A["tile_first"]).then_inc(s_first, 16)
                    if layer == 1:
                        sp.dma_start(SRC[:, :], A["src_tiles"]).then_inc(s_first, 16)
                    if layer == 1:
                        sp.dma_start(w_edge, A["W_edge"]).then_inc(s_prep, 16)
                        sp.wait_ge(s_zero, 1)
                        for h in range(H):
                            sp.dma_start(blockdiag[h * HD:(h + 1) * HD, h:h + 1],
                                         A["attn_edge"][h:h + 1, :].rearrange("a d -> d a")).then_inc(s_prep, 16)
                    sp.wait_ge(s_first, 16 * (1 + layer))

                    def step_sp(i):
                        starts = window_starts(sp, mybir.EngineType.SP, first, i)
                        for k in range(4):
                            g = i * 4 + k
                            done(sp, s_side, i, k - 4)
                            for j in range(GT):
                                sp.dma_start(window[k][:, j * win:(j + 1) * win], wtable[bass.ds(starts[k * GT + j], P), :]).then_inc(s_win[k], 16)
                            if layer == 1:
                                sp.dma_start(xe[k], A["xe_T"][:, bass.ds(g * GT * P, GT * P)]).then_inc(s_xe[k], 16)
                    loop(sp, G // 4, step_sp)

                @block.scalar
                def _(act):
                    def stage_index(i, k):
                        nc.scalar.copy(index[k % 4], cols(SRC, (i * 4 + k) * GT, GT)).then_inc(s_index[k % 4], 1)

                    act.wait_ge(s_first, 16 * (1 + layer))
                    for k in range(4):
                        stage_index(0, k)

                    def step_act(i, last):
                        for k in range(4):
                            done(act, s_T, i, k)
                            done(act, s_side, i, k - 2)
                            nc.scalar.copy(onehotT[k % 2], turned[k % 2]).then_inc(s_hotT[k % 2], 1)
                            done(act, s_got, i, k, 16 * GT)
                            kept = got[k].rearrange("p (t d) -> p t d", t=GT)[:, :, feat:feat + D]
                            to = gathered[bass.ds(i * 4 + k, 1), :, :].rearrange("a p (t d) -> (a p) t d", t=GT)
                            act.dma_start(to, kept).then_inc(s_kept[k], 16)
                            if not last:
                                stage_index(i, k + 4)
                    loop_ahead(act, G // 4, step_act)
                    for k in range(4):
                        act.wait_ge(s_kept[k], G // 4 * 16)

                @block.gpsimd
                def _(pool):
                    nc.gpsimd.memset(turn[:, 0:1], 0.0).then_inc(s_turn, 1)
                    pool.wait_ge(s_turn, 1)
                    def step_pool(i):
                        for k in range(4):
                            wait(pool, s_turn, i * 4 + k + 1)
                            done(pool, s_index, i, k)
                            done(pool, s_used, i, k - 4)
                            done(pool, s_kept, i, k - 4, 16)
                            nc.gpsimd.tensor_tensor(turn[:, 1:2], turn[:, 0:1], turn[:, 0:1], ALU.add).then_inc(s_turn, 1)
                            for j in range(GT):
                                pool.indirect_dma_start(out=got[k][:, j * row:(j + 1) * row], out_offset=None, in_=table,
                                                        in_offset=bass.IndirectOffsetOnAxis(ap=index[k][:, j:j + 1], axis=0)).then_inc(s_got[k], 16)
                    loop(pool, G // 4, step_pool)

                @block.tensor
                def _(pe):
                    if layer == 1:
                        pe.wait_ge(s_prep, 5 * 16)
                        nc.tensor.matmul(psum[4][:, 0:H], w_edge, blockdiag, start=True, stop=True).then_inc(s_w4, 1)
                        pe.wait_ge(s_w4, 2)

                    def transposes(i, k):
                        done(pe, s_hot, i, k)
                        done(pe, s_hotT, i, k - 2)
                        for j in range(GT):
                            last = nc.tensor.transpose(turned[k % 2][:, j * P:(j + 1) * P], onehot[k % 2][:, j * P:(j + 1) * P], eye[:, :])
                        last.then_inc(s_T[k % 2], 1)

                    def side(i, k):
                        done(pe, s_hotT, i, k)
                        done(pe, s_win, i, k, 16 * GT)
                        done(pe, s_used, i, k - 2)
                        bank, s = psum[2 + k % 2], k % 2
                        if layer == 1:
                            done(pe, s_xe, i, k, 16)
                        for j in range(GT):
                            hot = onehotT[s][:, j * P:(j + 1) * P]
                            if layer == 0:
                                last = nc.tensor.matmul(bank[:, j * D:(j + 1) * D], hot, window[k][:, j * D:(j + 1) * D], start=True, stop=True)
                            else:
                                nc.tensor.matmul(bank[:, j * win:(j + 1) * win], hot, window[k][:, j * win:(j + 1) * win], start=True, stop=True)
                                last = nc.tensor.matmul(bank[:, GT * win + j * H:GT * win + (j + 1) * H], xe[k][:, j * P:(j + 1) * P], w4, start=True, stop=True)
                        last.then_inc(s_side[k], 1)

                    transposes(0, 0)
                    def step_pe(i, last):
                        for k in range(4):
                            if not (last and k == 3):
                                transposes(i, k + 1)
                            side(i, k)
                    loop_ahead(pe, G // 4, step_pe)

                @block.vector
                def _(dve):
                    if layer == 1:
                        nc.vector.memset(blockdiag, 0.0).then_inc(s_zero, 1)
                        dve.wait_ge(s_w4, 1)
                        nc.vector.tensor_copy(w4, psum[4][:, 0:H]).then_inc(s_w4, 1)

                    def one_hots(i, k):
                        done(dve, s_T, i, k - 2)
                        rel = cols(REL, (i * 4 + k) * GT, GT).unsqueeze(2).broadcast_to([P, GT, P])
                        nc.vector.tensor_tensor(onehot[k % 2].rearrange("p (t n) -> p t n", t=GT), rel,
                                                iota_row[:, :].unsqueeze(1).broadcast_to([P, GT, P]), ALU.is_equal).then_inc(s_hot[k % 2], 1)

                    def logits(i, k):
                        done(dve, s_side, i, k)
                        done(dve, s_got, i, k, 16 * GT)
                        done(dve, s_log, i, k - 2)
                        rows = got[k].rearrange("p (t d) -> p t d", t=GT)
                        at, bank, w = (i * 4 + k) * GT * H, psum[2 + k % 2], work[k % 2]
                        if layer == 0:
                            nc.vector.tensor_tensor(w.rearrange("p (t d) -> p t d", t=GT), rows[:, :, 0:D],
                                                    bank[:, :].rearrange("p (t d) -> p t d", t=GT), ALU.mult).then_inc(s_used[k], 1)
                            done(dve, s_used, i, k)
                            nc.vector.tensor_reduce(cols(W1, at, GT * H), w.rearrange("p (a d) -> p a d", d=HD), AX, ALU.add).then_inc(s_log[k % 2], 1)
                        else:
                            w1, w2, e_dst = (w[:, n * GT * H:(n + 1) * GT * H] for n in range(3))
                            nc.vector.tensor_reduce(e_dst.rearrange("p (t h) -> p t h", t=GT),
                                                    bank[:, 0:GT * win].rearrange("p (t q h) -> p t h q", t=GT, q=3), AX, ALU.add).then_inc(s_part[k % 2], 1)
                            done(dve, s_part, i, k)
                            nc.vector.tensor_tensor(w2, e_dst, bank[:, GT * win:GT * (win + H)], ALU.add)
                            nc.vector.tensor_tensor(w1.rearrange("p (t h) -> p t h", t=GT), rows[:, :, D:D + H],
                                                    e_dst.rearrange("p (t h) -> p t h", t=GT), ALU.add).then_inc(s_used[k], 1)
                            done(dve, s_used, i, k)
                            nc.vector.scalar_tensor_tensor(cols(W1, at, GT * H), w1, SLOPE, w1, ALU.mult, ALU.max)
                            nc.vector.scalar_tensor_tensor(cols(W2, at, GT * H), w2, SLOPE, w2, ALU.mult, ALU.max).then_inc(s_log[k % 2], 1)

                    one_hots(0, 0)
                    def step_dve(i, last):
                        for k in range(4):
                            if not (last and k == 3):
                                one_hots(i, k + 1)
                            logits(i, k)
                    loop_ahead(dve, G // 4, step_dve)

        def transpose_all(name, src, dst):
            stage = SCR[:, SCR.shape[1] - GT * P:]
            s_stage, s_T, s_copied = (sem(f"{name}_{x}") for x in ("stage", "T", "copied"))
            with nc.Block() as block:
                @block.scalar
                def _(act):
                    def step_act(i):
                        wait(act, s_T, i)
                        nc.scalar.copy(stage, cols(src, i * GT * P, GT * P)).then_inc(s_stage, 1)
                    loop(act, C // GT, step_act)

                @block.tensor
                def _(pe):
                    def step_pe(i):
                        wait(pe, s_stage, i + 1)
                        wait(pe, s_copied, i)
                        for j in range(GT):
                            last = nc.tensor.transpose(psum[0][:, j * P:(j + 1) * P], stage[:, j * P:(j + 1) * P], ident[:, :])
                        last.then_inc(s_T, 1)
                    loop(pe, C // GT, step_pe)

                @block.vector
                def _(dve):
                    def step_dve(i):
                        wait(dve, s_T, i + 1)
                        nc.vector.tensor_copy(cols(dst, i * GT * P, GT * P), psum[0][:, :]).then_inc(s_copied, 1)
                    loop(dve, C // GT, step_dve)

        def edge_softmax(name, W, scale):
            carve = Carve()
            half = lambda: carve(SL // 2).bitcast(BF16)
            keep_prev, keep_next, head_part, tail_part = (half() for _ in range(4))
            cost_prev, cost_next, cost_head, cost_tail = (half() for _ in range(4))
            index = carve(SL)
            flags, carry, edge_f, edge_l = carve(2), carve(2), carve(1), carve(1)
            strip_keep, strip_cost = carve(2 * P), carve(2 * P)
            strip_f, strip_b = carve(P + 1), carve(P + 1)
            rows = SUM[:, 0:ET * H]
            heads = rows.rearrange("p (h n) -> p h n", h=H)
            fwd, bwd, prev_f, next_f = (SUM[:, (H + n) * SL:(H + n + 1) * SL] for n in (0, 1, 0, 1))
            prev_i, next_i = (SUM[:, (H + n) * SL:(H + n + 1) * SL].bitcast(I32) for n in range(2))
            s_dma, s_idx, s_heads, s_chain, s_ends, s_Tends, s_strips, s_Tstrips, s_sub, s_exp, s_weights, s_back = (
                sem(f"{name}_{x}") for x in ("dma", "idx", "heads", "chain", "ends", "Tends", "strips", "Tstrips",
                                             "sub", "exp", "weights", "back"))
            rows3 = rows.rearrange("p (c e) -> p c e", e=P)
            rows_of = lambda table: table.rearrange("(c r) e -> r c e", r=P)
            heads_of = lambda table, h: table.rearrange("(p t h) e -> h p t e", h=H, t=ST)[h]

            transpose_all(f"{name}_out", W, rows)
            with nc.Block() as block:
                @block.sync
                def _(sp):
                    line = A["dst_line"]
                    for n, to in ((0, prev_i), (1, index.bitcast(I32)), (2, next_i)):
                        sp.dma_start(to, line[n:n + EP].rearrange("(p n) -> p n", p=P)).then_inc(s_idx, 16)
                    sp.dma_start(rows_of(rows_out), rows3).then_inc(s_dma, 16)
                    sp.wait_ge(s_dma, 16)
                    for h in range(H):
                        sp.dma_start(heads[:, h, :].rearrange("p (t e) -> p t e", e=P), heads_of(rows_out, h)).then_inc(s_heads, 16)
                    for h in range(H):
                        sp.wait_ge(s_weights, h + 1)
                        sp.dma_start(heads_of(rows_in, h), heads[:, h, :].rearrange("p (t e) -> p t e", e=P)).then_inc(s_dma, 16)
                    sp.wait_ge(s_dma, (1 + H) * 16)
                    sp.dma_start(rows3, rows_of(rows_in)).then_inc(s_back, 16)
                    sp.wait_ge(s_back, 16)

                @block.vector
                def _(dve):
                    link = chained(dve, s_chain)
                    v, turns = nc.vector, [0]
                    dve.wait_ge(s_idx, 3 * 16)
                    link(v.tensor_copy(index, index.bitcast(I32)))
                    link(v.tensor_copy(prev_f, prev_i))
                    link(v.tensor_copy(next_f, next_i))
                    link(v.tensor_tensor(keep_prev, prev_f, index, ALU.is_equal))
                    link(v.tensor_tensor(keep_next, next_f, index, ALU.is_equal))
                    link(v.tensor_tensor(edge_f, keep_prev[:, 0:1], keep_prev[:, 0:1], ALU.mult))
                    link(v.tensor_tensor(edge_l, keep_next[:, SL - 1:SL], keep_next[:, SL - 1:SL], ALU.mult))
                    link(v.tensor_scalar(head_part, index, index[:, 0:1], edge_f, ALU.is_equal, ALU.mult))
                    link(v.tensor_scalar(tail_part, index, index[:, SL - 1:SL], edge_l, ALU.is_equal, ALU.mult))
                    for flag, cost in ((keep_prev, cost_prev), (keep_next, cost_next), (head_part, cost_head), (tail_part, cost_tail)):
                        link(v.tensor_scalar(cost, flag, 1.0, BIG, ALU.subtract, ALU.mult))
                    link(v.tensor_reduce(flags[:, 0:1], keep_prev, AX, ALU.min))
                    v.tensor_reduce(flags[:, 1:2], keep_next, AX, ALU.min).then_inc(s_ends, 1)
                    turns[0] = 1
                    dve.wait_ge(s_Tends, 1)
                    link(v.tensor_copy(strip_keep[0:1, :], psum[0][0:1, 0:2 * P]))
                    link(v.tensor_scalar(strip_cost[0:1, :], strip_keep[0:1, :], 1.0, BIG, ALU.subtract, ALU.mult))
                    dve.wait_ge(s_heads, H * 16)

                    def carries(per_strip, none, op0, op1):
                        turns[0] += 1
                        dve.sem_inc(s_ends, 1)
                        dve.wait_ge(s_Tends, turns[0])
                        link(v.memset(strip_f[0:1, 0:1], none))
                        link(v.memset(strip_b[0:1, P:P + 1], none))
                        link(v.tensor_tensor_scan(strip_f[0:1, 1:P + 1], per_strip[0:1, 0:P], psum[0][0:1, 0:P], none, op0, op1))
                        v.tensor_tensor_scan(strip_b[0:1, 0:P][:, ::-1], per_strip[0:1, P:2 * P][:, ::-1],
                                             psum[0][0:1, P:2 * P][:, ::-1], none, op0, op1).then_inc(s_strips, 1)
                        dve.wait_ge(s_Tstrips, turns[0] - 1)
                        link(v.tensor_copy(carry, psum[1][:, 0:2]))

                    for h in range(H):
                        a = heads[:, h, :]
                        link(v.tensor_tensor_scan(fwd, cost_prev, a, -BIG, ALU.add, ALU.max))
                        link(v.tensor_tensor_scan(bwd[:, ::-1], cost_next[:, ::-1], a[:, ::-1], -BIG, ALU.add, ALU.max))
                        carries(strip_cost, -BIG, ALU.add, ALU.max)
                        link(v.scalar_tensor_tensor(fwd, cost_head, carry[:, 0:1], fwd, ALU.add, ALU.max))
                        link(v.scalar_tensor_tensor(bwd, cost_tail, carry[:, 1:2], bwd, ALU.add, ALU.max))
                        link(v.tensor_tensor(fwd, fwd, bwd, ALU.max))
                        v.tensor_tensor(a, a, fwd, ALU.subtract).then_inc(s_sub, 1)
                        dve.wait_ge(s_exp, h + 1)
                        link(v.tensor_tensor_scan(fwd, keep_prev, a, 0.0, ALU.mult, ALU.add))
                        link(v.tensor_tensor_scan(bwd[:, ::-1], keep_next[:, ::-1], a[:, ::-1], 0.0, ALU.mult, ALU.add))
                        carries(strip_keep, 0.0, ALU.mult, ALU.add)
                        link(v.scalar_tensor_tensor(fwd, head_part, carry[:, 0:1], fwd, ALU.mult, ALU.add))
                        link(v.scalar_tensor_tensor(bwd, tail_part, carry[:, 1:2], bwd, ALU.mult, ALU.add))
                        link(v.tensor_tensor(bwd, bwd, a, ALU.subtract))
                        link(v.tensor_tensor(fwd, fwd, bwd, ALU.add))
                        link(v.reciprocal(fwd, fwd))
                        v.tensor_tensor(a, a, fwd, ALU.mult).then_inc(s_weights, 1)
                        dve.wait_ge(s_weights, h + 1)

                @block.scalar
                def _(act):
                    for h in range(H):
                        act.wait_ge(s_sub, h + 1)
                        nc.scalar.activation(heads[:, h, :], heads[:, h, :], ACT.Exp, scale=scale).then_inc(s_exp, 1)

                @block.tensor
                def _(pe):
                    for n in range(1 + 2 * H):
                        ends = (flags[:, 0:1], flags[:, 1:2]) if n == 0 else (fwd[:, SL - 1:SL], bwd[:, 0:1])
                        pe.wait_ge(s_ends, n + 1)
                        nc.tensor.transpose(psum[0][0:1, 0:P], ends[0], ident[:, :])
                        nc.tensor.transpose(psum[0][0:1, P:2 * P], ends[1], ident[:, :]).then_inc(s_Tends, 1)
                        if n:
                            pe.wait_ge(s_strips, n)
                            nc.tensor.transpose(psum[1][:, 0:1], strip_f[0:1, 0:P], ident[0:1, 0:1])
                            nc.tensor.transpose(psum[1][:, 1:2], strip_b[0:1, 1:P + 1], ident[0:1, 0:1]).then_inc(s_Tstrips, 1)
            transpose_all(f"{name}_in", rows, W)

        def pass_b(layer):
            name = f"b{layer}"
            carve = Carve()
            kept = [carve(GT * D) for _ in range(4)]
            onehot, msg = ([carve(GT * P) for _ in range(2)] for _ in range(2))
            apart = [carve(GT * P) for _ in range(2)]
            if layer == 1:
                xe, total = ([carve(GT * P) for _ in range(n)] for n in (4, 2))
                w_edge_T = carve(D)
            first = SRC[0:1, :]
            s_first = sem(f"{name}_first")
            s_kept = sems(f"{name}_kept", 4)
            s_msg = sems(f"{name}_msg", 4)
            s_hot, s_sum, s_apart = (sems(f"{name}_{x}", 2) for x in ("onehot", "sum", "apart"))
            s_add, s_zero = (sem(f"{name}_{x}") for x in ("add", "zero"))
            if layer == 1:
                s_xe, s_he = (sems(f"{name}_{x}", 4) for x in ("xedge", "hedge"))
                s_me, s_total = (sems(f"{name}_{x}", 2) for x in ("msgedge", "total"))
            s_read = s_sum if layer == 0 else s_total
            full = msg if layer == 0 else total
            with nc.Block() as block:
                @block.sync
                def _(sp):
                    sp.dma_start(first, A["tile_first"]).then_inc(s_first, 16)
                    if layer == 1:
                        sp.dma_start(w_edge_T, A["W_edge_T"]).then_inc(s_first, 16)
                    def step_sp(i):
                        for k in range(4):
                            g = i * 4 + k
                            done(sp, s_msg, i, k - 4)
                            sp.dma_start(kept[k], gathered[bass.ds(g, 1), :, :].rearrange("a p n -> (a p) n")).then_inc(s_kept[k], 16)
                            if layer == 1:
                                done(sp, s_he, i, k - 4)
                                sp.dma_start(xe[k], A["xe_T"][:, bass.ds(g * GT * P, GT * P)]).then_inc(s_xe[k], 16)
                    loop(sp, G // 4, step_sp)

                by_head = lambda t: t.rearrange("p (a d) -> p a d", d=HD)

                def weights_of(t, i, k):
                    return cols(t, (i * 4 + k) * GT * H, GT * H).unsqueeze(2).broadcast_to([P, GT * H, HD])

                @block.scalar
                def _(act):
                    def distances(i, k):
                        done(act, s_hot, i, k - 2)
                        for j in range(GT):
                            last = nc.scalar.activation(apart[k % 2][:, j * P:(j + 1) * P], iota_row[:, :], ACT.Abs, scale=-1.0,
                                                        bias=cols(REL, (i * 4 + k) * GT + j, 1))
                        last.then_inc(s_apart[k % 2], 1)

                    distances(0, 0)
                    def step_act(i, last):
                        for k in range(4):
                            if not (last and k == 3):
                                distances(i, k + 1)
                            done(act, s_apart, i, k)
                            done(act, s_sum, i, k - 2)
                            nc.scalar.activation(onehot[k % 2], apart[k % 2], ACT.Relu, scale=-1.0, bias=1.0).then_inc(s_hot[k % 2], 1)
                    loop_ahead(act, G // 4, step_act)

                @block.gpsimd
                def _(pool):
                    def step_pool(i):
                        for k in range(4):
                            done(pool, s_kept, i, k, 16)
                            done(pool, s_read, i, k - 2, 1 + layer)
                            nc.gpsimd.tensor_tensor(by_head(msg[k % 2]), by_head(kept[k]), weights_of(W1, i, k), ALU.mult).then_inc(s_msg[k], 1)
                    loop(pool, G // 4, step_pool)

                @block.tensor
                def _(pe):
                    def edges(i, k):
                        done(pe, s_xe, i, k, 16)
                        done(pe, s_me, i, k - 2, 2)
                        for j in range(GT):
                            last = nc.tensor.matmul(psum[4 + k % 2][:, j * D:(j + 1) * D], xe[k % 4][:, j * P:(j + 1) * P], w_edge_T, start=True, stop=True)
                        last.then_inc(s_he[k % 4], 1)

                    if layer == 1:
                        pe.wait_ge(s_first, 32)
                    if layer == 1:
                        edges(0, 0)
                        edges(0, 1)
                    def step_pe(i, last_turn):
                        for k in range(4):
                            if layer == 1 and not (last_turn and k >= 2):
                                edges(i, k + 2)
                            done(pe, s_hot, i, k)
                            done(pe, s_msg, i, k) if layer == 0 else done(pe, s_total, i, k, 2)
                            wait(pe, s_add, (i * 4 + k - 1) * GT)
                            for j in range(GT):
                                last = nc.tensor.matmul(psum[k % 2][:, j * P:(j + 1) * P], full[k % 2][:, j * D:(j + 1) * D],
                                                        onehot[k % 2][:, j * P:(j + 1) * P], start=True, stop=True)
                            last.then_inc(s_sum[k % 2], 1)
                    loop_ahead(pe, G // 4, step_pe)

                @block.vector
                def _(dve):
                    nc.vector.memset(SUM[:, :], 0.0).then_inc(s_zero, 1)
                    dve.wait_ge(s_zero, 1)
                    dve.wait_ge(s_first, 32 if layer == 1 else 16)

                    def halves(t, n):
                        return by_head(t[:, n * GT * D // 2:(n + 1) * GT * D // 2])

                    def edge_messages(i, k, n):
                        if n == 0:
                            done(dve, s_he, i, k)
                            done(dve, s_sum, i, k - 2)
                        at = ((i * 4 + k) * 2 + n) * GT * H // 2
                        weights = cols(W2, at, GT * H // 2).unsqueeze(2).broadcast_to([P, GT * H // 2, HD])
                        nc.vector.tensor_tensor(halves(total[k % 2], n), halves(psum[4 + k % 2], n), weights, ALU.mult).then_inc(s_me[k % 2], 1)

                    def all_messages(i, k, n):
                        if n == 0:
                            done(dve, s_msg, i, k)
                        done(dve, s_me, i, k, 2, 1 - n)
                        t = halves(total[k % 2], n)
                        nc.vector.tensor_tensor(t, t, halves(msg[k % 2], n), ALU.add).then_inc(s_total[k % 2], 1)

                    def add(i, k, j, starts):
                        t = (i * 4 + k) * GT + j
                        wait(dve, s_add, t)
                        w = SUM[:, bass.ds(starts[k * GT + j], P)]
                        nc.vector.tensor_tensor(w, w, psum[k % 2][:, j * P:(j + 1) * P], ALU.add).then_inc(s_add, 1)

                    between = [(edge_messages, 0), (edge_messages, 1), (all_messages, 0), (all_messages, 1)]
                    if layer == 1:
                        for k in range(2):
                            for step, n in between:
                                step(0, k, n)

                    def step_dve(i, last):
                        starts = window_starts(dve, mybir.EngineType.DVE, first, i)
                        for k in range(4):
                            done(dve, s_sum, i, k)
                            for j, (step, n) in enumerate(between):
                                add(i, k, j, starts)
                                if layer == 1 and not (last and k >= 2):
                                    step(i, k + 2, n)
                    loop_ahead(dve, G // 4, step_dve)

        def sums_to_rows(name, onto_x):
            carve = Carve()
            stage = [carve(P) for _ in range(2)]
            s_stage, s_T, s_copied = (sems(f"{name}_{x}", 2) for x in ("stage", "T", "copied"))
            with nc.Block() as block:
                @block.scalar
                def _(act):
                    def step_act(i):
                        for s in range(2):
                            wait(act, s_T[s], i)
                            nc.scalar.copy(stage[s], cols(SUM, (i * 2 + s) * P, P)).then_inc(s_stage[s], 1)
                    loop(act, NT // 2, step_act)

                @block.tensor
                def _(pe):
                    def step_pe(i):
                        for s in range(2):
                            wait(pe, s_stage[s], i + 1)
                            wait(pe, s_copied[s], i)
                            nc.tensor.transpose(psum[s][:, 0:P], stage[s], ident[:, :]).then_inc(s_T[s], 1)
                    loop(pe, NT // 2, step_pe)

                @block.vector
                def _(dve):
                    def step_dve(i):
                        for s in range(2):
                            wait(dve, s_T[s], i + 1)
                            if onto_x:
                                x = X[:, bass.ds(i * 2 + s, 1), :].rearrange("p a d -> p (a d)")
                                nc.vector.tensor_tensor(x, x, psum[s][:, 0:P], ALU.add).then_inc(s_copied[s], 1)
                            else:
                                nc.vector.tensor_copy(cols(SUM, (i * 2 + s) * P, P), psum[s][:, 0:P]).then_inc(s_copied[s], 1)
                    loop(dve, NT // 2, step_dve)

        def gate_and_norm():
            chunk_tiles = max(n for n in range(1, NT + 1) if NT % n == 0 and n * D <= SCR.shape[1] // 2)
            carve = Carve()
            tmp = carve(chunk_tiles * D)
            wg, gamma, beta = carve(3 * D), carve(D), carve(D)
            z, dev, var, mean = carve(NT), carve(NT), carve(NT), carve(NT)
            stats = carve(6 * NT)
            alpha, neg_bg = carve(1), carve(1)
            skip = W[:, 0:NP]
            s_load, s_chain, s_z, s_e, s_stats, s_var, s_std = (sem(f"g_{x}") for x in ("load", "chain", "z", "e", "stats", "var", "std"))
            t3 = lambda t: t.rearrange("p (t d) -> p t d", d=D)
            with nc.Block() as block:
                @block.sync
                def _(sp):
                    sp.dma_start(t3(skip), skip_table.rearrange("(t p) d -> p t d", p=P)).then_inc(s_load, 16)
                    for to, of in ((wg, A["Wg"].rearrange("n a -> (n a)")), (gamma, A["gamma"]), (beta, A["beta"]), (alpha, A["alpha"]), (neg_bg, A["bg"])):
                        sp.dma_start(to, of.partition_broadcast(P)).then_inc(s_load, 16)
                    sp.wait_ge(s_load, 6 * 16)

                @block.scalar
                def _(act):
                    act.wait_ge(s_z, 1)
                    nc.scalar.activation(z, z, ACT.Exp, scale=-1.0).then_inc(s_e, 1)
                    act.wait_ge(s_var, 1)
                    nc.scalar.activation(var, var, ACT.Sqrt).then_inc(s_std, 1)

                @block.vector
                def _(dve):
                    link, v = chained(dve, s_chain), nc.vector
                    over = lambda row, n: row.unsqueeze(1).broadcast_to([P, n, D])
                    spread = lambda col, n: col.unsqueeze(2).broadcast_to([P, n, D])
                    dve.wait_ge(s_load, 6 * 16)
                    for c in range(NT // chunk_tiles):
                        n = chunk_tiles
                        sl, ts = slice(c * n * D, (c + 1) * n * D), slice(c * n, (c + 1) * n)
                        sk, agg = skip[:, sl], SUM[:, sl]
                        link(v.tensor_tensor(t3(tmp), t3(sk), over(wg[:, 0:D], n), ALU.mult))
                        link(v.tensor_reduce(z[:, ts], t3(tmp), AX, ALU.add))
                        link(v.tensor_tensor(t3(tmp), t3(agg), over(wg[:, D:2 * D], n), ALU.mult))
                        link(v.tensor_reduce(var[:, ts], t3(tmp), AX, ALU.add))
                        link(v.tensor_tensor(sk, sk, agg, ALU.subtract))
                        link(v.tensor_tensor(t3(tmp), t3(sk), over(wg[:, 2 * D:3 * D], n), ALU.mult))
                        link(v.tensor_reduce(dev[:, ts], t3(tmp), AX, ALU.add))
                    link(v.tensor_tensor(z, z, var, ALU.add))
                    link(v.scalar_tensor_tensor(z, z, neg_bg, dev, ALU.add, ALU.add))
                    dve.sem_inc(s_z, 1)
                    dve.wait_ge(s_e, 1)
                    link(v.tensor_scalar(z, z, 1.0, None, ALU.add))
                    link(v.reciprocal(z, z))
                    link(v.tensor_tensor(t3(skip), t3(skip), spread(z, NT), ALU.mult))
                    link(v.tensor_tensor(SUM[:, :], SUM[:, :], skip, ALU.add))
                    st = stats.rearrange("p (t k) -> p t k", k=6)
                    for t in range(NT):
                        v.bn_stats(stats[:, 6 * t:6 * t + 6], SUM[:, t * D:(t + 1) * D]).then_inc(s_stats, 1)
                    dve.wait_ge(s_stats, NT)
                    moments(link, st, mean, dev, var, s_var)
                    dve.wait_ge(s_std, 1)
                    link(v.reciprocal(var, var))
                    link(v.tensor_tensor(t3(SUM[:, :]), t3(SUM[:, :]), spread(mean, NT), ALU.subtract))
                    link(v.tensor_tensor(t3(SUM[:, :]), t3(SUM[:, :]), spread(var, NT), ALU.mult))
                    link(v.tensor_tensor(t3(SUM[:, :]), t3(SUM[:, :]), over(gamma, NT), ALU.mult))
                    link(v.tensor_tensor(t3(SUM[:, :]), t3(SUM[:, :]), over(beta, NT), ALU.add))
                    link(v.tensor_scalar(skip, SUM[:, :], 0.0, alpha, ALU.min, ALU.mult))
                    link(v.scalar_tensor_tensor(SUM[:, :], SUM[:, :], 0.0, skip, ALU.max, ALU.add))
                    flat = X[:, :, :].rearrange("p t d -> p (t d)")
                    link(v.tensor_tensor(flat, flat, SUM[:, :], ALU.add))

        def store():
            s_stored = sem("o_stored")
            whole, rest = n_nodes // P, n_nodes % P
            with nc.Block() as block:
                @block.sync
                def _(sp):
                    sp.dma_start(A["out"][0:whole * P, :].rearrange("(t p) d -> p t d", p=P), X[:, 0:whole, :]).then_inc(s_stored, 16)
                    if rest:
                        sp.dma_start(A["out"][whole * P:n_nodes, :], X[0:rest, whole, :]).then_inc(s_stored, 16)
                    sp.wait_ge(s_stored, 16 * (2 if rest else 1))

        phase(setup)
        phase(node_tables, 0)
        phase(pass_a, 0)
        phase(edge_softmax, "s0", W1, float(HD) ** -0.5)
        phase(pass_b, 0)
        phase(sums_to_rows, "r0", False)
        phase(gate_and_norm)
        phase(node_tables, 1)
        phase(pass_a, 1)
        phase(edge_softmax, "s1", W1, 1.0)
        phase(edge_softmax, "s2", W2, 1.0)
        phase(pass_b, 1)
        phase(sums_to_rows, "r1", True)
        phase(store)


def kernel(x, src, dst, edge_attr_128, L0_gnn_Wq, L0_gnn_bq, L0_gnn_Wk, L0_gnn_bk, L0_gnn_Wv, L0_gnn_bv,
           L0_gnn_Ws, L0_gnn_bs, L0_gnn_Wg, L0_gnn_bg, L0_gnn_gamma, L0_gnn_beta, L0_gnn_alpha,
           L1_gnn_W_src, L1_gnn_W_dst, L1_gnn_W_edge, L1_gnn_attn_src, L1_gnn_attn_dst, L1_gnn_attn_edge):
    import concourse.bacc as bacc
    from concourse.bass_utils import run_bass_kernel_spmd

    n_nodes, n_edges = x.shape[0], src.shape[0]
    NT, ET = sizes(n_nodes, n_edges)
    ep = ET * P
    f = lambda a: np.asarray(a)
    x_pad = np.zeros((NT * P, D), np.float32)
    x_pad[:n_nodes] = f(x)
    src_pad = np.zeros(ep, np.int32)
    src_pad[:n_edges] = f(src)
    dst_line = np.full(ep + 2, -1, np.int32)
    dst_line[1:n_edges + 1] = f(dst)
    dst_line[n_edges + 1:ep + 1] = n_nodes
    dst_pad = dst_line[1:-1]
    xe_T = np.zeros((D, ep), np.float32)
    xe_T[:, :n_edges] = f(edge_attr_128).T
    arrays = {
        "x": x_pad, "xe_T": xe_T, "dst_line": dst_line,
        "src_tiles": src_pad.reshape(ET, P).T, "dst_tiles": dst_pad.reshape(ET, P).T,
        "tile_first": dst_pad.reshape(ET, P)[:, 0].reshape(1, ET),
        "Wq": f(L0_gnn_Wq), "Wk": f(L0_gnn_Wk), "Wv": f(L0_gnn_Wv), "Ws": f(L0_gnn_Ws),
        "bq": f(L0_gnn_bq), "bk": f(L0_gnn_bk), "bv": f(L0_gnn_bv), "bs": f(L0_gnn_bs),
        "Wg": f(L0_gnn_Wg), "bg": f(L0_gnn_bg), "gamma": f(L0_gnn_gamma), "beta": f(L0_gnn_beta),
        "alpha": f(L0_gnn_alpha).reshape(1),
        "W_src_T": f(L1_gnn_W_src).T, "W_dst_T": f(L1_gnn_W_dst).T, "W_edge": f(L1_gnn_W_edge), "W_edge_T": f(L1_gnn_W_edge).T,
        "attn_src": f(L1_gnn_attn_src), "attn_dst": f(L1_gnn_attn_dst), "attn_edge": f(L1_gnn_attn_edge),
    }
    nc = bacc.Bacc("TRN2", target_bir_lowering=False, num_devices=1)
    ins, A = {}, {}
    for name, a in arrays.items():
        a = np.ascontiguousarray(a)
        ins[f"in_{name}"] = a
        A[name] = nc.dram_tensor(f"in_{name}", a.shape, mybir.dt.from_np(a.dtype), kind="ExternalInput").ap()
    A["out"] = nc.dram_tensor("out", (n_nodes, D), F32, kind="ExternalOutput").ap()
    build(nc, A, n_nodes, n_edges)
    r = run_bass_kernel_spmd(nc, [ins], core_ids=[0])
    return r.results[0]["out"]
```

```python
from contextlib import ExitStack

import numpy as np

import concourse.bass as bass
from concourse import mybir
from concourse.alu_op_type import AluOpType as ALU

ACT = mybir.ActivationFunctionType
AX = mybir.AxisListType.X
F32 = mybir.dt.float32
I32 = mybir.dt.int32
BF16 = mybir.dt.bfloat16

P = 128
D = 128
H = 4
HD = D // H
GT = 4
NS = 4
CT = P // H
EPS = 1e-5
SLOPE = 0.2
BIG = 1e30


def sizes(n_nodes, n_edges):
    node_tiles = -(-(n_nodes + 2 * P) // P)
    node_tiles += -node_tiles % NS
    unit = P * P
    return node_tiles, -(-n_edges // unit) * P


def build(nc, A, n_nodes, n_edges):
    NT, ET = sizes(n_nodes, n_edges)
    NP = NT * P
    EP = ET * P
    G = ET // GT
    C = ET // CT
    ST = ET // P
    SL = ST * P
    assert G % 4 == 0 and G >= 12 and ET * H == C * P and C % GT == 0 and NP + NT <= 2 * ET * H and 7 * SL <= NP

    def dram(name, shape, dt=F32):
        return nc.dram_tensor(name, shape, dt, kind="Internal").ap()

    qv_table = dram("qv_table", (NP, 2 * D))
    ks_table = dram("ks_table", (NP, 2 * D))
    hs_table = dram("hs_table", (NP, D + H))
    ed_table = dram("ed_table", (NP, 3 * H), BF16)
    gathered = dram("gathered", (G, P, GT * D))
    rows_out = [dram(f"rows_out{n}", (ET * H, P)) for n in range(2)]
    rows_in = [dram(f"rows_in{n}", (ET * H, P)) for n in range(2)]

    with ExitStack() as ctx:
        def sb(name, shape, dt=F32):
            return ctx.enter_context(nc.sbuf_tensor(name, shape, dt))

        phase_sems = []

        def sem(name):
            phase_sems.append(nc.alloc_semaphore(name=name))
            return phase_sems[-1]

        def phase(program, *args):
            program(*args)
            nc.clear_and_free_semaphores(phase_sems)
            nc.all_engine_barrier()
            phase_sems.clear()

        def sems(name, n):
            return [sem(f"{name}{i}") for i in range(n)]

        X = sb("X", [P, NT, D])
        SUM = sb("SUM", [P, NP])
        W = sb("W", [P, 2 * ET * H])
        W1, W2 = W[:, 0:ET * H], W[:, ET * H:2 * ET * H]
        REL = sb("REL", [P, ET])
        z_agg = W[:, NP:NP + NT]
        SRC = sb("SRC", [P, ET], I32)
        SCR = sb("SCR", [P, 9472])
        ident = sb("ident", [P, P])
        ident_b = sb("ident_b", [P, P], BF16)
        iota_row = sb("iota_row", [P, 2 * P])
        psum = [ctx.enter_context(nc.psum_tensor(f"bank{i}", [P, 512], F32)) for i in range(8)]

        class Carve:
            def __init__(self):
                self.at = 0

            def __call__(self, n):
                self.at += n
                assert self.at <= SCR.shape[1], self.at
                return SCR[:, self.at - n:self.at]

        def chained(eng, s):
            count = [0]

            def link(ins):
                count[0] += 1
                ins.then_inc(s, 1)
                eng.wait_ge(s, count[0])
            return link

        def wait(eng, s, value):
            if not isinstance(value, int) or value > 0:
                eng.wait_ge(s, value)

        def done(eng, s, i, k, each=1, less=0):
            n = len(s)
            wait(eng, s[k % n], (i * (4 // n) + k // n + 1) * each - less)

        def loop(eng, n, body):
            body(0)
            if n > 1:
                with eng.Fori(1, n) as i:
                    body(i)

        def loop_ahead(eng, n, body):
            body(0, False)
            if n > 2:
                with eng.Fori(1, n - 1) as i:
                    body(i, False)
            body(n - 1, True)

        def window_starts(engine, first, at, n):
            return nc.values_load_multi_w_load_instructions(first[0:1, bass.ds(at, n)], engines=[engine],
                                                            min_val=0, max_val=n_nodes,
                                                            skip_runtime_bounds_check_because="every dst is a node, or the padding's row")[1]

        def cols(t, start, n):
            return t[:, bass.ds(start, n)]

        def setup():
            s_load, s_const, s_iota = sem("set_load"), sem("set_const"), sem("set_iota")
            s_chain = sem("set_chain")
            dst_i = SUM[:, 0:ET].bitcast(I32)
            first_i = SUM[:, ET:2 * ET].bitcast(I32)
            iota_i = SUM[:, 2 * ET:2 * ET + 2 * P].bitcast(I32)
            with nc.Block() as block:
                @block.sync
                def _(sp):
                    sp.dma_start(SRC[:, :], A["src_tiles"]).then_inc(s_load, 16)
                    sp.dma_start(dst_i, A["dst_tiles"]).then_inc(s_load, 16)
                    sp.dma_start(first_i, A["tile_first"].partition_broadcast(P)).then_inc(s_load, 16)
                    for c in range(2):
                        ts = slice(c * NT // 2, (c + 1) * NT // 2)
                        sp.dma_start(X[:, ts, :], A["x"].rearrange("(t p) d -> p t d", p=P)[:, ts, :]).then_inc(s_load, 16)
                    sp.wait_ge(s_load, 5 * 16)

                @block.gpsimd
                def _(pool):
                    pool.memset(ident[:, :], 0.0).then_inc(s_const, 1)
                    pool.iota(iota_i, pattern=[[1, 2 * P]], base=0, channel_multiplier=0).then_inc(s_iota, 1)
                    pool.wait_ge(s_const, 1)
                    pool.affine_select(out=ident[:, :], in_=ident[:, :], compare_op=ALU.not_equal, fill=1.0,
                                       base=0, pattern=[[-1, P]], channel_multiplier=1).then_inc(s_const, 1)

                @block.vector
                def _(dve):
                    link = chained(dve, s_chain)
                    dve.wait_ge(s_iota, 1)
                    link(nc.vector.tensor_copy(iota_row[:, :], iota_i))
                    dve.wait_ge(s_const, 2)
                    link(nc.vector.tensor_copy(ident_b[:, :], ident[:, :]))
                    dve.wait_ge(s_load, 5 * 16)
                    link(nc.vector.tensor_tensor(REL[:, :], dst_i, first_i, ALU.subtract))

        def moments(link, st, mean, dev, var, s_var):
            link(nc.vector.tensor_tensor(mean, st[:, :, 1], st[:, :, 4], ALU.add))
            link(nc.vector.tensor_scalar(mean, mean, 0.5, None, ALU.mult))
            link(nc.vector.tensor_tensor(dev, st[:, :, 1], st[:, :, 4], ALU.subtract))
            link(nc.vector.tensor_scalar(dev, dev, 0.5, None, ALU.mult))
            link(nc.vector.tensor_tensor(dev, dev, dev, ALU.mult))
            link(nc.vector.tensor_tensor(var, st[:, :, 2], st[:, :, 5], ALU.add))
            link(nc.vector.tensor_scalar(var, var, 1.0 / D, EPS, ALU.mult, ALU.add))
            nc.vector.tensor_tensor(var, var, dev, ALU.add).then_inc(s_var, 1)

        def norm_stats(name, stats, scale_out, shift_out, tmp):
            s_stats, s_chain, s_var, s_std = (sem(f"{name}_{x}") for x in ("stats", "chain", "var", "std"))
            st = stats.rearrange("p (t k) -> p t k", k=6)
            with nc.Block() as block:
                @block.vector
                def _(dve):
                    link = chained(dve, s_chain)
                    def step_dve(i):
                        for k in range(NS):
                            t = bass.ds(i * NS + k, 1)
                            nc.vector.bn_stats(st[:, t, :].rearrange("p a k -> p (a k)"),
                                               X[:, t, :].rearrange("p a d -> p (a d)")).then_inc(s_stats, 1)
                    loop(dve, NT // NS, step_dve)
                    dve.wait_ge(s_stats, NT)
                    mean, dev, var = tmp[:, 0:NT], tmp[:, NT:2 * NT], tmp[:, 2 * NT:3 * NT]
                    moments(link, st, mean, dev, var, s_var)
                    dve.wait_ge(s_std, 1)
                    link(nc.vector.reciprocal(scale_out, var))
                    link(nc.vector.scalar_tensor_tensor(shift_out, mean, -1.0, scale_out, ALU.mult, ALU.mult))

                @block.scalar
                def _(act):
                    act.wait_ge(s_var, 1)
                    var = tmp[:, 2 * NT:3 * NT]
                    nc.scalar.activation(var, var, ACT.Sqrt).then_inc(s_std, 1)


        def node_tables(layer):
            name = f"t{layer}"
            width = 4 * D if layer == 0 else 2 * (D + H)
            carve = Carve()
            stats, tmp = carve(6 * NT), carve(3 * NT)
            scale, shift = carve(NT), carve(NT)
            weights = carve(width)
            h, hT = ([carve(D) for _ in range(NS)] for _ in range(2))
            out = [carve(4 * D if layer == 0 else D + H) for _ in range(NS)]
            norm_stats(f"n{layer}", stats, scale, shift, tmp)
            s_w = sem(f"{name}_weights")
            s_h, s_T, s_hT, s_mm, s_out, s_stored, s_free = (
                sems(f"{name}_{x}", NS) for x in ("h", "T", "hT", "mm", "out", "stored", "free"))
            if layer == 0:
                biases = carve(width)
                loads = [(weights[:, n * D:(n + 1) * D], A[w]) for n, w in enumerate(("Wq", "Wv", "Wk", "Ws"))]
                loads += [(biases[:, n * D:(n + 1) * D], A[b].partition_broadcast(P)) for n, b in enumerate(("bq", "bv", "bk", "bs"))]
                stores = lambda rows, o: [(qv_table[rows, :], o[:, 0:2 * D]), (ks_table[rows, :], o[:, 2 * D:4 * D])]
            else:
                E = D + H
                w_plain, blockdiag = ([carve(n) for _ in range(2)] for n in (D, H))
                loads = [(weights[:, n * E:n * E + D], A[w]) for n, w in enumerate(("W_src_T", "W_dst_T"))]
                loads += [(w_plain[n], A[w]) for n, w in enumerate(("W_src", "W_dst"))]
                heads_loads = [(blockdiag[n][h * HD:(h + 1) * HD, h:h + 1], A[w][h:h + 1, :].rearrange("a d -> d a"))
                               for n, w in enumerate(("attn_src", "attn_dst")) for h in range(H)]
                s_zero, s_heads, s_we, s_ready = (sem(f"{name}_{x}") for x in ("zero", "heads", "we", "ready"))
                stores = lambda rows, o: [(hs_table[rows, :], o[:, 0:D + H])]
                e_dst, split = carve(NT * H), carve(NT * H * 3 // 2)
                parts = split.bitcast(BF16).rearrange("p (t q h) -> p t q h", q=3, h=H)
                s_split, s_parts = sem(f"{name}_split"), sem(f"{name}_parts")
            each = 16 * (2 if layer == 0 else 1)
            with nc.Block() as block:
                @block.sync
                def _(sp):
                    for to, of in loads:
                        sp.dma_start(to, of).then_inc(s_w, 16)
                    if layer == 1:
                        sp.wait_ge(s_zero, 1)
                        for to, of in heads_loads:
                            sp.dma_start(to, of).then_inc(s_heads, 16)
                    def step_sp(i):
                        for s in range(NS):
                            wait(sp, s_out[s], i + 1)
                            for to, of in stores(bass.ds((i * NS + s) * P, P), out[s]):
                                sp.dma_start(to, of).then_inc(s_stored[s], 16)
                    loop(sp, NT // NS, step_sp)
                    for s in range(NS):
                        sp.wait_ge(s_stored[s], NT // NS * each)
                    if layer == 1:
                        sp.wait_ge(s_split, 5)
                        sp.dma_start(ed_table.rearrange("(t p) n -> p t n", p=P), parts.rearrange("p t q h -> p t (q h)")).then_inc(s_parts, 16)
                        sp.wait_ge(s_parts, 16)

                @block.scalar
                def _(act):
                    def normalise(t, s):
                        nc.scalar.activation(h[s], X[:, bass.ds(t, 1), :].rearrange("p a d -> p (a d)"),
                                             ACT.Relu, bias=cols(shift, t, 1), scale=cols(scale, t, 1)).then_inc(s_h[s], 1)

                    for s in range(NS):
                        normalise(s, s)
                    def step_act(i, last):
                        for s in range(NS):
                            wait(act, s_T[s], i + 1)
                            wait(act, s_mm[s], i)
                            nc.scalar.copy(hT[s], psum[s][:, 0:D]).then_inc(s_hT[s], 1)
                            if not last:
                                normalise((i + 1) * NS + s, s)
                    loop_ahead(act, NT // NS, step_act)

                @block.tensor
                def _(pe):
                    pe.wait_ge(s_w, len(loads) * 16)
                    if layer == 1:
                        pe.wait_ge(s_heads, len(heads_loads) * 16)
                        for n in range(2):
                            nc.tensor.matmul(psum[NS][:, n * H:(n + 1) * H], w_plain[n], blockdiag[n], start=True, stop=True).then_inc(s_we, 1)
                        pe.wait_ge(s_ready, 1)
                    for s in range(NS):
                        pe.wait_ge(s_h[s], 1)
                        nc.tensor.transpose(psum[s][:, 0:D], h[s], ident[:, :]).then_inc(s_T[s], 1)
                    def step_pe(i, last):
                        for s in range(NS):
                            wait(pe, s_hT[s], i + 1)
                            if not last:
                                wait(pe, s_h[s], i + 2)
                                nc.tensor.transpose(psum[s][:, 0:D], h[s], ident[:, :]).then_inc(s_T[s], 1)
                            wait(pe, s_free[s], i)
                            nc.tensor.matmul(psum[NS + s][:, 0:width], hT[s], weights, start=True, stop=True).then_inc(s_mm[s], 1)
                    loop_ahead(pe, NT // NS, step_pe)

                @block.vector
                def _(dve):
                    if layer == 1:
                        nc.vector.memset(blockdiag[0], 0.0)
                        nc.vector.memset(blockdiag[1], 0.0).then_inc(s_zero, 1)
                        dve.wait_ge(s_we, 2)
                        nc.vector.tensor_copy(weights.rearrange("p (n e) -> p n e", n=2)[:, :, D:E],
                                              psum[NS][:, 0:2 * H].rearrange("p (n h) -> p n h", n=2)).then_inc(s_ready, 1)
                    dve.wait_ge(s_w, len(loads) * 16)
                    def step_dve(i):
                        for s in range(NS):
                            bank, o = psum[NS + s], out[s]
                            wait(dve, s_mm[s], i + 1)
                            wait(dve, s_stored[s], i * each)
                            if layer == 0:
                                nc.vector.tensor_tensor(o, bank[:, :], biases, ALU.add).then_inc(s_out[s], 1)
                                wait(dve, s_out[s], i + 1)
                                dve.sem_inc(s_free[s], 1)
                            else:
                                at = X[:, bass.ds(i * NS + s, 1), :].rearrange("p a d -> p (a d)")
                                nc.vector.tensor_copy(o, bank[:, 0:E]).then_inc(s_out[s], 1)
                                nc.vector.tensor_tensor(at, at, bank[:, E:E + D], ALU.add)
                                nc.vector.tensor_copy(cols(e_dst, (i * NS + s) * H, H), bank[:, E + D:2 * E]).then_inc(s_free[s], 1)
                    loop(dve, NT // NS, step_dve)
                    if layer == 1:
                        dve.wait_ge(s_free[NS - 1], NT // NS)
                        left = e_dst.rearrange("p (t h) -> p t h", h=H)
                        for q in range(3):
                            nc.vector.tensor_copy(parts[:, :, q, :], left).then_inc(s_split, 1)
                            if q < 2:
                                dve.wait_ge(s_split, 2 * q + 1)
                                nc.vector.tensor_tensor(left, left, parts[:, :, q, :], ALU.subtract).then_inc(s_split, 1)
                                dve.wait_ge(s_split, 2 * q + 2)

        def pass_a(layer):
            name = f"a{layer}"
            row = 2 * D if layer == 0 else D + H
            feat = D if layer == 0 else 0
            win = D if layer == 0 else 3 * H
            eye = ident if layer == 0 else ident_b
            table = qv_table if layer == 0 else hs_table
            wtable = ks_table[:, 0:D] if layer == 0 else ed_table
            carve = Carve()
            got = [carve(GT * row) for _ in range(4)]
            def carve_hot(n):
                return carve(n) if layer == 0 else carve(n // 2).bitcast(BF16)

            window = [carve_hot(GT * win) for _ in range(4)]
            onehot, onehotT = ([carve_hot(GT * P) for _ in range(2)] for _ in range(2))
            turned = [psum[s][:, :] if layer == 0 else psum[s][:, 0:GT * P // 2].bitcast(BF16) for s in range(2)]
            work = [carve(GT * D if layer == 0 else 3 * GT * H) for _ in range(2)]
            index = [carve(GT).bitcast(I32) for _ in range(4)]
            xe = [carve(GT * P) for _ in range(4)] if layer == 1 else None
            if layer == 1:
                w_edge, blockdiag, w4 = carve(D), carve(H), carve(H)
            turn = carve(2)[0:1, :]
            first = SUM[0:1, 0:ET].bitcast(I32)
            s_first, s_prep, s_w4, s_zero, s_turn = (sem(f"{name}_{x}") for x in ("first", "prep", "w4", "zero", "turn"))
            s_index, s_got, s_kept, s_used = (sems(f"{name}_{x}", 4) for x in ("index", "got", "kept", "used"))
            s_win, s_side = (sems(f"{name}_{x}", 4) for x in ("window", "side"))
            s_hot, s_T, s_hotT, s_log = (sems(f"{name}_{x}", 2) for x in ("onehot", "T", "onehotT", "logits"))
            if layer == 1:
                s_xe, s_part = sems(f"{name}_xedge", 4), sems(f"{name}_part", 2)

            with nc.Block() as block:
                @block.sync
                def _(sp):
                    sp.dma_start(first, A["tile_first"]).then_inc(s_first, 16)
                    if layer == 1:
                        sp.dma_start(SRC[:, :], A["src_tiles"]).then_inc(s_first, 16)
                        sp.dma_start(w_edge, A["W_edge"]).then_inc(s_prep, 16)
                        sp.wait_ge(s_zero, 1)
                        for h in range(H):
                            sp.dma_start(blockdiag[h * HD:(h + 1) * HD, h:h + 1],
                                         A["attn_edge"][h:h + 1, :].rearrange("a d -> d a")).then_inc(s_prep, 16)
                    sp.wait_ge(s_first, 16 * (1 + layer))

                    def step_sp(i):
                        starts = window_starts(mybir.EngineType.SP, first, i * 4 * GT, 4 * GT)
                        for k in range(4):
                            g = i * 4 + k
                            done(sp, s_side, i, k - 4)
                            for j in range(GT):
                                sp.dma_start(window[k][:, j * win:(j + 1) * win], wtable[bass.ds(starts[k * GT + j], P), :]).then_inc(s_win[k], 16)
                            if layer == 1:
                                sp.dma_start(xe[k], A["xe_T"][:, bass.ds(g * GT * P, GT * P)]).then_inc(s_xe[k], 16)
                    loop(sp, G // 4, step_sp)

                @block.scalar
                def _(act):
                    def stage_index(i, k):
                        nc.scalar.copy(index[k % 4], cols(SRC, (i * 4 + k) * GT, GT)).then_inc(s_index[k % 4], 1)

                    act.wait_ge(s_first, 16 * (1 + layer))
                    for k in range(4):
                        stage_index(0, k)

                    def step_act(i, last):
                        for k in range(4):
                            done(act, s_T, i, k)
                            done(act, s_side, i, k - 2)
                            nc.scalar.copy(onehotT[k % 2], turned[k % 2]).then_inc(s_hotT[k % 2], 1)
                            done(act, s_got, i, k, 16 * GT)
                            kept = got[k].rearrange("p (t d) -> p t d", t=GT)[:, :, feat:feat + D]
                            to = gathered[bass.ds(i * 4 + k, 1), :, :].rearrange("a p (t d) -> (a p) t d", t=GT)
                            act.dma_start(to, kept).then_inc(s_kept[k], 16)
                            if not last:
                                stage_index(i, k + 4)
                    loop_ahead(act, G // 4, step_act)
                    for k in range(4):
                        act.wait_ge(s_kept[k], G // 4 * 16)

                @block.gpsimd
                def _(pool):
                    nc.gpsimd.memset(turn[:, 0:1], 0.0).then_inc(s_turn, 1)
                    pool.wait_ge(s_turn, 1)
                    def step_pool(i):
                        for k in range(4):
                            wait(pool, s_turn, i * 4 + k + 1)
                            done(pool, s_index, i, k)
                            done(pool, s_used, i, k - 4)
                            done(pool, s_kept, i, k - 4, 16)
                            nc.gpsimd.tensor_tensor(turn[:, 1:2], turn[:, 0:1], turn[:, 0:1], ALU.add).then_inc(s_turn, 1)
                            for j in range(GT):
                                pool.indirect_dma_start(out=got[k][:, j * row:(j + 1) * row], out_offset=None, in_=table,
                                                        in_offset=bass.IndirectOffsetOnAxis(ap=index[k][:, j:j + 1], axis=0)).then_inc(s_got[k], 16)
                    loop(pool, G // 4, step_pool)

                @block.tensor
                def _(pe):
                    if layer == 1:
                        pe.wait_ge(s_prep, 5 * 16)
                        nc.tensor.matmul(psum[4][:, 0:H], w_edge, blockdiag, start=True, stop=True).then_inc(s_w4, 1)
                        pe.wait_ge(s_w4, 2)

                    def transposes(i, k):
                        done(pe, s_hot, i, k)
                        done(pe, s_hotT, i, k - 2)
                        for j in range(GT):
                            last = nc.tensor.transpose(turned[k % 2][:, j * P:(j + 1) * P], onehot[k % 2][:, j * P:(j + 1) * P], eye[:, :])
                        last.then_inc(s_T[k % 2], 1)

                    def side(i, k):
                        done(pe, s_hotT, i, k)
                        done(pe, s_win, i, k, 16 * GT)
                        done(pe, s_used, i, k - 2)
                        bank, s = psum[2 + k % 2], k % 2
                        if layer == 1:
                            done(pe, s_xe, i, k, 16)
                        for j in range(GT):
                            hot = onehotT[s][:, j * P:(j + 1) * P]
                            if layer == 0:
                                last = nc.tensor.matmul(bank[:, j * D:(j + 1) * D], hot, window[k][:, j * D:(j + 1) * D], start=True, stop=True)
                            else:
                                nc.tensor.matmul(bank[:, j * win:(j + 1) * win], hot, window[k][:, j * win:(j + 1) * win], start=True, stop=True)
                                last = nc.tensor.matmul(bank[:, GT * win + j * H:GT * win + (j + 1) * H], xe[k][:, j * P:(j + 1) * P], w4, start=True, stop=True)
                        last.then_inc(s_side[k], 1)

                    transposes(0, 0)
                    def step_pe(i, last):
                        for k in range(4):
                            if not (last and k == 3):
                                transposes(i, k + 1)
                            side(i, k)
                    loop_ahead(pe, G // 4, step_pe)

                @block.vector
                def _(dve):
                    if layer == 1:
                        nc.vector.memset(blockdiag, 0.0).then_inc(s_zero, 1)
                        dve.wait_ge(s_w4, 1)
                        nc.vector.tensor_copy(w4, psum[4][:, 0:H]).then_inc(s_w4, 1)

                    def one_hots(i, k):
                        done(dve, s_T, i, k - 2)
                        rel = cols(REL, (i * 4 + k) * GT, GT).unsqueeze(2).broadcast_to([P, GT, P])
                        nc.vector.tensor_tensor(onehot[k % 2].rearrange("p (t n) -> p t n", t=GT), rel,
                                                iota_row[:, 0:P].unsqueeze(1).broadcast_to([P, GT, P]), ALU.is_equal).then_inc(s_hot[k % 2], 1)

                    def logits(i, k):
                        done(dve, s_side, i, k)
                        done(dve, s_got, i, k, 16 * GT)
                        done(dve, s_log, i, k - 2)
                        rows = got[k].rearrange("p (t d) -> p t d", t=GT)
                        at, bank, w = (i * 4 + k) * GT * H, psum[2 + k % 2], work[k % 2]
                        if layer == 0:
                            nc.vector.tensor_tensor(w.rearrange("p (t d) -> p t d", t=GT), rows[:, :, 0:D],
                                                    bank[:, :].rearrange("p (t d) -> p t d", t=GT), ALU.mult).then_inc(s_used[k], 1)
                            done(dve, s_used, i, k)
                            nc.vector.tensor_reduce(cols(W1, at, GT * H), w.rearrange("p (a d) -> p a d", d=HD), AX, ALU.add).then_inc(s_log[k % 2], 1)
                        else:
                            w1, w2, e_dst = (w[:, n * GT * H:(n + 1) * GT * H] for n in range(3))
                            nc.vector.tensor_reduce(e_dst.rearrange("p (t h) -> p t h", t=GT),
                                                    bank[:, 0:GT * win].rearrange("p (t q h) -> p t h q", t=GT, q=3), AX, ALU.add).then_inc(s_part[k % 2], 1)
                            done(dve, s_part, i, k)
                            nc.vector.tensor_tensor(w2, e_dst, bank[:, GT * win:GT * (win + H)], ALU.add)
                            nc.vector.tensor_tensor(w1.rearrange("p (t h) -> p t h", t=GT), rows[:, :, D:D + H],
                                                    e_dst.rearrange("p (t h) -> p t h", t=GT), ALU.add).then_inc(s_used[k], 1)
                            done(dve, s_used, i, k)
                            nc.vector.scalar_tensor_tensor(cols(W1, at, GT * H), w1, SLOPE, w1, ALU.mult, ALU.max)
                            nc.vector.scalar_tensor_tensor(cols(W2, at, GT * H), w2, SLOPE, w2, ALU.mult, ALU.max).then_inc(s_log[k % 2], 1)

                    one_hots(0, 0)
                    def step_dve(i, last):
                        for k in range(4):
                            if not (last and k == 3):
                                one_hots(i, k + 1)
                            logits(i, k)
                    loop_ahead(dve, G // 4, step_dve)

        def transpose_all(name, src, dst):
            half = GT // 2 * P
            stage = [SCR[:, SCR.shape[1] - (n + 1) * half:SCR.shape[1] - n * half] for n in range(2)]
            s_stage, s_T, s_copied = (sems(f"{name}_{x}", 2) for x in ("stage", "T", "copied"))
            with nc.Block() as block:
                @block.scalar
                def _(act):
                    def step_act(i):
                        for n in range(2):
                            wait(act, s_T[n], i)
                            nc.scalar.copy(stage[n], cols(src, (i * 2 + n) * half, half)).then_inc(s_stage[n], 1)
                    loop(act, C // GT, step_act)

                @block.tensor
                def _(pe):
                    def step_pe(i):
                        for n in range(2):
                            wait(pe, s_stage[n], i + 1)
                            wait(pe, s_copied[n], i)
                            for j in range(GT // 2):
                                last = nc.tensor.transpose(psum[n][:, j * P:(j + 1) * P], stage[n][:, j * P:(j + 1) * P], ident[:, :])
                            last.then_inc(s_T[n], 1)
                    loop(pe, C // GT, step_pe)

                @block.vector
                def _(dve):
                    def step_dve(i):
                        for n in range(2):
                            wait(dve, s_T[n], i + 1)
                            nc.vector.tensor_copy(cols(dst, (i * 2 + n) * half, half), psum[n][:, 0:half]).then_inc(s_copied[n], 1)
                    loop(dve, C // GT, step_dve)

        def edge_softmax(name, logits, scale):
            carve = Carve()
            half = lambda: carve(SL // 2).bitcast(BF16)
            keep_prev, keep_next, head_part, tail_part = (half() for _ in range(4))
            cost_prev, cost_next, cost_head, cost_tail = (half() for _ in range(4))
            index = carve(SL)
            flags, edge_f, edge_l = carve(2), carve(1), carve(1)
            strip_keep, strip_cost = carve(2 * P), carve(2 * P)
            MAX, TOTAL = 0, 1
            carry, strip_f, strip_b = ([carve(n) for _ in range(2)] for n in (2, P + 1, P + 1))
            place = [SUM[:, 0:ET * H], W1]
            N = len(logits) * H
            head = [place[n // H][:, n % H * SL:(n % H + 1) * SL] for n in range(N)]
            slots = [SUM[:, (H + n) * SL:(H + n + 1) * SL] for n in range(3)] + [index]
            prev_f, next_f = slots[0:2]
            prev_i, next_i = (t.bitcast(I32) for t in slots[0:2])
            s_rows, s_idx, s_stored, s_chain, s_flags, s_Tflags, s_sub, s_exp, s_less, s_inv, s_weights, s_top, s_both, s_total = (
                sem(f"{name}_{x}") for x in ("rows", "idx", "stored", "chain", "flags", "Tflags", "sub", "exp", "less",
                                             "inv", "weights", "top", "both", "total"))
            s_heads, s_back = sems(f"{name}_heads", len(logits)), sem(f"{name}_back")
            s_ends, s_Tends, s_strips, s_Tstrips = (sems(f"{name}_{x}", 2) for x in ("ends", "Tends", "strips", "Tstrips"))
            rows3 = [p.rearrange("p (c e) -> p c e", e=P) for p in place]
            rows_of = lambda table: table.rearrange("(c r) e -> r c e", r=P)
            head_of = lambda table, h: table.rearrange("(p t h) e -> h p t e", h=H, t=ST)[h]
            by_tile = lambda t: t.rearrange("p (t e) -> p t e", e=P)

            for n, W in enumerate(logits):
                transpose_all(f"{name}_out{n}", W, place[n])
            with nc.Block() as block:
                @block.sync
                def _(sp):
                    line = A["dst_line"]
                    for n, to in ((0, prev_i), (1, index.bitcast(I32)), (2, next_i)):
                        sp.dma_start(to, line[n:n + EP].rearrange("(p n) -> p n", p=P)).then_inc(s_idx, 16)
                    for n in range(len(logits)):
                        sp.dma_start(rows_of(rows_out[n]), rows3[n]).then_inc(s_rows, 16)
                    sp.wait_ge(s_rows, len(logits) * 16)
                    for n in range(N):
                        sp.dma_start(by_tile(head[n]), head_of(rows_out[n // H], n % H)).then_inc(s_heads[n // H], 16)
                    for n in range(N):
                        sp.wait_ge(s_weights, n + 1)
                        sp.dma_start(head_of(rows_in[n // H], n % H), by_tile(head[n])).then_inc(s_stored, 16)
                        if n % H == H - 1:
                            sp.wait_ge(s_stored, (n + 1) * 16)
                            sp.dma_start(rows3[n // H], rows_of(rows_in[n // H])).then_inc(s_back, 16)
                    sp.wait_ge(s_back, len(logits) * 16)

                @block.vector
                def _(dve):
                    link, v = chained(dve, s_chain), nc.vector
                    dve.wait_ge(s_idx, 3 * 16)
                    link(v.tensor_copy(index, index.bitcast(I32)))
                    link(v.tensor_copy(prev_f, prev_i))
                    link(v.tensor_copy(next_f, next_i))
                    link(v.tensor_tensor(keep_prev, prev_f, index, ALU.is_equal))
                    link(v.tensor_tensor(keep_next, next_f, index, ALU.is_equal))
                    link(v.tensor_tensor(edge_f, keep_prev[:, 0:1], keep_prev[:, 0:1], ALU.mult))
                    link(v.tensor_tensor(edge_l, keep_next[:, SL - 1:SL], keep_next[:, SL - 1:SL], ALU.mult))
                    link(v.tensor_scalar(head_part, index, index[:, 0:1], edge_f, ALU.is_equal, ALU.mult))
                    link(v.tensor_scalar(tail_part, index, index[:, SL - 1:SL], edge_l, ALU.is_equal, ALU.mult))
                    for flag, cost in ((keep_prev, cost_prev), (keep_next, cost_next), (head_part, cost_head), (tail_part, cost_tail)):
                        link(v.tensor_scalar(cost, flag, 1.0, BIG, ALU.subtract, ALU.mult))
                    link(v.tensor_reduce(flags[:, 0:1], keep_prev, AX, ALU.min))
                    v.tensor_reduce(flags[:, 1:2], keep_next, AX, ALU.min).then_inc(s_flags, 1)
                    dve.wait_ge(s_Tflags, 1)
                    link(v.tensor_copy(strip_keep[0:1, :], psum[4][0:1, 0:2 * P]))
                    link(v.tensor_scalar(strip_cost[0:1, :], strip_keep[0:1, :], 1.0, BIG, ALU.subtract, ALU.mult))

                    def scans(kind, n):
                        a, fwd, bwd = head[n], slots[n % 2 * 2], slots[n % 2 * 2 + 1]
                        flag_f, flag_b, none, op0, op1 = (cost_prev, cost_next, -BIG, ALU.add, ALU.max) if kind == MAX else \
                                                         (keep_prev, keep_next, 0.0, ALU.mult, ALU.add)
                        if kind == MAX:
                            dve.wait_ge(s_heads[n // H], H * 16)
                            if n >= 2:
                                dve.wait_ge(s_weights, n - 1)
                        else:
                            dve.wait_ge(s_exp, n + 1)
                        link(v.tensor_tensor_scan(fwd, flag_f, a, none, op0, op1))
                        v.tensor_tensor_scan(bwd[:, ::-1], flag_b[:, ::-1], a[:, ::-1], none, op0, op1).then_inc(s_ends[kind], 1)

                    def over_strips(kind, n):
                        per_strip, none, op0, op1 = (strip_cost, -BIG, ALU.add, ALU.max) if kind == MAX else (strip_keep, 0.0, ALU.mult, ALU.add)
                        ends, f, b = psum[2 * kind], strip_f[kind], strip_b[kind]
                        dve.wait_ge(s_Tends[kind], n + 1)
                        if n == 0:
                            link(v.memset(f[0:1, 0:1], none))
                            link(v.memset(b[0:1, P:P + 1], none))
                        link(v.tensor_tensor_scan(f[0:1, 1:P + 1], per_strip[0:1, 0:P], ends[0:1, 0:P], none, op0, op1))
                        v.tensor_tensor_scan(b[0:1, 0:P][:, ::-1], per_strip[0:1, P:2 * P][:, ::-1],
                                             ends[0:1, P:2 * P][:, ::-1], none, op0, op1).then_inc(s_strips[kind], 1)

                    def take_over(kind, n):
                        fwd, bwd, c = slots[n % 2 * 2], slots[n % 2 * 2 + 1], carry[kind]
                        dve.wait_ge(s_Tstrips[kind], n + 1)
                        link(v.tensor_copy(c, psum[2 * kind + 1][:, 0:2]))
                        if kind == MAX:
                            link(v.scalar_tensor_tensor(fwd, cost_head, c[:, 0:1], fwd, ALU.add, ALU.max))
                            link(v.scalar_tensor_tensor(bwd, cost_tail, c[:, 1:2], bwd, ALU.add, ALU.max))
                            v.tensor_tensor(fwd, fwd, bwd, ALU.max).then_inc(s_top, 1)
                        else:
                            link(v.scalar_tensor_tensor(fwd, head_part, c[:, 0:1], fwd, ALU.mult, ALU.add))
                            dve.wait_ge(s_less, n + 1)
                            v.scalar_tensor_tensor(bwd, tail_part, c[:, 1:2], bwd, ALU.mult, ALU.add).then_inc(s_both, 1)

                    def invert(n):
                        total = slots[n % 2 * 2]
                        dve.wait_ge(s_total, n + 1)
                        v.reciprocal(total, total).then_inc(s_inv, 1)

                    scans(MAX, 0)
                    over_strips(MAX, 0)
                    take_over(MAX, 0)
                    for n in range(N):
                        scans(TOTAL, n)
                        if n + 1 < N:
                            scans(MAX, n + 1)
                        over_strips(TOTAL, n)
                        if n + 1 < N:
                            over_strips(MAX, n + 1)
                        take_over(TOTAL, n)
                        if n + 1 < N:
                            take_over(MAX, n + 1)
                        invert(n)

                @block.scalar
                def _(act):
                    for n in range(N):
                        act.wait_ge(s_sub, n + 1)
                        nc.scalar.activation(head[n], head[n], ACT.Exp, scale=scale).then_inc(s_exp, 1)

                @block.gpsimd
                def _(pool):
                    def less_top(n):
                        pool.wait_ge(s_top, n + 1)
                        nc.gpsimd.tensor_tensor(head[n], head[n], slots[n % 2 * 2], ALU.subtract).then_inc(s_sub, 1)

                    less_top(0)
                    for n in range(N):
                        bwd = slots[n % 2 * 2 + 1]
                        pool.wait_ge(s_Tends[TOTAL], n + 1)
                        nc.gpsimd.tensor_tensor(bwd, bwd, head[n], ALU.subtract).then_inc(s_less, 1)
                        pool.wait_ge(s_both, n + 1)
                        nc.gpsimd.tensor_tensor(slots[n % 2 * 2], slots[n % 2 * 2], bwd, ALU.add).then_inc(s_total, 1)
                        if n + 1 < N:
                            less_top(n + 1)
                        pool.wait_ge(s_inv, n + 1)
                        nc.gpsimd.tensor_tensor(head[n], head[n], slots[n % 2 * 2], ALU.mult).then_inc(s_weights, 1)

                @block.tensor
                def _(pe):
                    def turn_ends(bank, first_end, last_end, s):
                        nc.tensor.transpose(bank[0:1, 0:P], first_end, ident[:, :])
                        nc.tensor.transpose(bank[0:1, P:2 * P], last_end, ident[:, :]).then_inc(s, 1)

                    def ends(kind, n):
                        pe.wait_ge(s_ends[kind], n + 1)
                        turn_ends(psum[2 * kind], slots[n % 2 * 2][:, SL - 1:SL], slots[n % 2 * 2 + 1][:, 0:1], s_Tends[kind])

                    def strips(kind, n):
                        pe.wait_ge(s_strips[kind], n + 1)
                        bank = psum[2 * kind + 1]
                        nc.tensor.transpose(bank[:, 0:1], strip_f[kind][0:1, 0:P], ident[0:1, 0:1])
                        nc.tensor.transpose(bank[:, 1:2], strip_b[kind][0:1, 1:P + 1], ident[0:1, 0:1]).then_inc(s_Tstrips[kind], 1)

                    pe.wait_ge(s_flags, 1)
                    turn_ends(psum[4], flags[:, 0:1], flags[:, 1:2], s_Tflags)
                    ends(MAX, 0)
                    strips(MAX, 0)
                    for n in range(N):
                        ends(TOTAL, n)
                        if n + 1 < N:
                            ends(MAX, n + 1)
                        strips(TOTAL, n)
                        if n + 1 < N:
                            strips(MAX, n + 1)
            for n, W in reversed(list(enumerate(logits))):
                transpose_all(f"{name}_in{n}", place[n], W)

        def pass_b(layer):
            name = f"b{layer}"
            carve = Carve()
            kept = [carve(GT * D) for _ in range(4)]
            PAIRS = GT // 2
            msg = [carve(GT * P) for _ in range(2)]
            onehot = [carve(3 * PAIRS * P) for _ in range(2)]
            narrow = lambda t, q: t[:, q * P:(q + 1) * P]
            wide = lambda t, q: t[:, (PAIRS + 2 * q) * P:(PAIRS + 2 * q + 2) * P]
            hot_width = (1 if layer == 0 else 3) * PAIRS * P
            apart = [carve(hot_width) for _ in range(2)]
            if layer == 1:
                xe, total = ([carve(GT * P) for _ in range(n)] for n in (4, 2))
                w_edge_T = carve(D)
            first = SRC[0:1, :].rearrange("p (a two) -> p a two", two=2)[:, :, 0]
            of_pairs = lambda t: t[:, :].rearrange("p (a two) -> p a two", two=2)
            firsts = of_pairs(SRC)
            shift = carve(ET // 2) if layer == 0 else SUM[:, 0:ET // 2]
            s_first = sem(f"{name}_first")
            s_kept = sems(f"{name}_kept", 4)
            s_msg = sems(f"{name}_msg", 4)
            s_hot, s_sum, s_apart = (sems(f"{name}_{x}", 2) for x in ("onehot", "sum", "apart"))
            s_wide = sems(f"{name}_wide", 2) if layer == 0 else None
            s_add, s_zero, s_rel = (sem(f"{name}_{x}") for x in ("add", "zero", "rel"))
            if layer == 1:
                s_xe, s_he = (sems(f"{name}_{x}", 4) for x in ("xedge", "hedge"))
                s_me, s_total = (sems(f"{name}_{x}", 2) for x in ("msgedge", "total"))
            s_read = s_sum if layer == 0 else s_total
            full = msg if layer == 0 else total
            with nc.Block() as block:
                @block.sync
                def _(sp):
                    sp.dma_start(SRC[:, :], A["tile_first"].partition_broadcast(P)).then_inc(s_first, 16)
                    if layer == 1:
                        sp.dma_start(w_edge_T, A["W_edge_T"]).then_inc(s_first, 16)
                    def step_sp(i):
                        for k in range(4):
                            g = i * 4 + k
                            done(sp, s_msg, i, k - 4)
                            sp.dma_start(kept[k], gathered[bass.ds(g, 1), :, :].rearrange("a p n -> (a p) n")).then_inc(s_kept[k], 16)
                            if layer == 1:
                                done(sp, s_he, i, k - 4)
                                sp.dma_start(xe[k], A["xe_T"][:, bass.ds(g * GT * P, GT * P)]).then_inc(s_xe[k], 16)
                    loop(sp, G // 4, step_sp)

                by_head = lambda t: t.rearrange("p (a d) -> p a d", d=HD)

                def weights_of(t, i, k):
                    return cols(t, (i * 4 + k) * GT * H, GT * H).unsqueeze(2).broadcast_to([P, GT * H, HD])

                @block.scalar
                def _(act):
                    def distances(i, k):
                        done(act, s_hot, i, k - 2)
                        for q in range(PAIRS):
                            for j, part, n in ((0, narrow, P), (1, wide, 2 * P)):
                                if j == 0 or layer == 1:
                                    last = nc.scalar.activation(part(apart[k % 2], q), iota_row[:, 0:n], ACT.Abs, scale=-1.0,
                                                                bias=cols(REL, (i * 4 + k) * GT + 2 * q + j, 1))
                        last.then_inc(s_apart[k % 2], 1)

                    act.wait_ge(s_rel, 1)
                    distances(0, 0)
                    def step_act(i, last):
                        for k in range(4):
                            if not (last and k == 3):
                                distances(i, k + 1)
                            done(act, s_apart, i, k)
                            done(act, s_sum, i, k - 2)
                            nc.scalar.activation(onehot[k % 2][:, 0:hot_width], apart[k % 2], ACT.Relu, scale=-1.0, bias=1.0).then_inc(s_hot[k % 2], 1)
                    loop_ahead(act, G // 4, step_act)

                @block.gpsimd
                def _(pool):
                    def step_pool(i):
                        for k in range(4):
                            done(pool, s_kept, i, k, 16)
                            done(pool, s_read, i, k - 2, 1 + layer)
                            nc.gpsimd.tensor_tensor(by_head(msg[k % 2]), by_head(kept[k]), weights_of(W1, i, k), ALU.mult).then_inc(s_msg[k], 1)
                    loop(pool, G // 4, step_pool)

                @block.tensor
                def _(pe):
                    def edges(i, k):
                        done(pe, s_xe, i, k, 16)
                        done(pe, s_me, i, k - 2, 2)
                        for j in range(GT):
                            last = nc.tensor.matmul(psum[4 + k % 2][:, j * D:(j + 1) * D], xe[k % 4][:, j * P:(j + 1) * P], w_edge_T, start=True, stop=True)
                        last.then_inc(s_he[k % 4], 1)

                    if layer == 1:
                        pe.wait_ge(s_first, 32)
                    if layer == 1:
                        edges(0, 0)
                        edges(0, 1)
                    def step_pe(i, last_turn):
                        for k in range(4):
                            if layer == 1 and not (last_turn and k >= 2):
                                edges(i, k + 2)
                            done(pe, s_hot, i, k)
                            done(pe, s_msg, i, k) if layer == 0 else done(pe, s_total, i, k, 2)
                            if layer == 0:
                                done(pe, s_wide, i, k)
                            wait(pe, s_add, (i * 4 + k - 3) * PAIRS)
                            for q in range(PAIRS):
                                window, rows = psum[k][:, 2 * q * P:2 * (q + 1) * P], full[k % 2]
                                nc.tensor.matmul(window, rows[:, (2 * q + 1) * D:(2 * q + 2) * D], wide(onehot[k % 2], q), start=True, stop=False)
                                last = nc.tensor.matmul(window[:, 0:P], rows[:, 2 * q * D:(2 * q + 1) * D], narrow(onehot[k % 2], q), start=False, stop=True)
                            last.then_inc(s_sum[k % 2], 1)
                    loop_ahead(pe, G // 4, step_pe)

                @block.vector
                def _(dve):
                    dve.wait_ge(s_first, 32 if layer == 1 else 16)
                    nc.vector.tensor_tensor(shift, firsts[:, :, 1], firsts[:, :, 0], ALU.subtract).then_inc(s_zero, 1)
                    dve.wait_ge(s_zero, 1)
                    second = of_pairs(REL)[:, :, 1]
                    nc.vector.tensor_tensor(second, second, shift, ALU.add).then_inc(s_rel, 1)
                    dve.wait_ge(s_rel, 1)
                    nc.vector.memset(SUM[:, :], 0.0).then_inc(s_zero, 1)
                    dve.wait_ge(s_zero, 2)

                    def halves(t, n):
                        return by_head(t[:, n * GT * D // 2:(n + 1) * GT * D // 2])

                    def edge_messages(i, k, n):
                        if n == 0:
                            done(dve, s_he, i, k)
                            done(dve, s_sum, i, k - 2)
                        at = ((i * 4 + k) * 2 + n) * GT * H // 2
                        weights = cols(W2, at, GT * H // 2).unsqueeze(2).broadcast_to([P, GT * H // 2, HD])
                        nc.vector.tensor_tensor(halves(total[k % 2], n), halves(psum[4 + k % 2], n), weights, ALU.mult).then_inc(s_me[k % 2], 1)

                    def all_messages(i, k, n):
                        if n == 0:
                            done(dve, s_msg, i, k)
                        done(dve, s_me, i, k, 2, 1 - n)
                        t = halves(total[k % 2], n)
                        nc.vector.tensor_tensor(t, t, halves(msg[k % 2], n), ALU.add).then_inc(s_total[k % 2], 1)

                    def wide_one_hots(i, k, n):
                        done(dve, s_sum, i, k - 2)
                        rel = cols(REL, (i * 4 + k) * GT, GT).rearrange("p (a two) -> p a two", two=2)[:, :, 1:2].broadcast_to([P, PAIRS, 2 * P])
                        nc.vector.tensor_tensor(onehot[k % 2][:, PAIRS * P:].rearrange("p (a n) -> p a n", n=2 * P), rel,
                                                iota_row[:, :].unsqueeze(1).broadcast_to([P, PAIRS, 2 * P]), ALU.is_equal).then_inc(s_wide[k % 2], 1)

                    def add(i, k, q, starts):
                        wait(dve, s_add, (i * 4 + k) * PAIRS + q)
                        w = SUM[:, bass.ds(starts[k * PAIRS + q], 2 * P)]
                        nc.vector.tensor_tensor(w, w, psum[k][:, 2 * q * P:2 * (q + 1) * P], ALU.add).then_inc(s_add, 1)

                    between = [[(wide_one_hots, 0)], []] if layer == 0 else [[(edge_messages, 0), (edge_messages, 1)], [(all_messages, 0), (all_messages, 1)]]
                    for k in range(2):
                        for step, n in between[0] + between[1]:
                            step(0, k, n)

                    def step_dve(i, last):
                        starts = window_starts(mybir.EngineType.DVE, first, i * 4 * PAIRS, 4 * PAIRS)
                        for k in range(4):
                            done(dve, s_sum, i, k)
                            for q in range(PAIRS):
                                add(i, k, q, starts)
                                if not (last and k >= 2):
                                    for step, n in between[q]:
                                        step(i, k + 2, n)
                    loop_ahead(dve, G // 4, step_dve)
                    if layer == 0:
                        nc.vector.tensor_tensor(second, second, shift, ALU.subtract).then_inc(s_rel, 1)

        def sums_to_rows(name, onto_x):
            carve = Carve()
            stage = [carve(P) for _ in range(NS)]
            wg2, wg3, wg_agg = carve(1), carve(1), carve(1)
            s_wg, s_diff = sem(f"{name}_wg"), sem(f"{name}_diff")
            s_stage, s_T, s_copied = (sems(f"{name}_{x}", NS) for x in ("stage", "T", "copied"))
            with nc.Block() as block:
                if not onto_x:
                    @block.sync
                    def _(sp):
                        for n, to in ((1, wg2), (2, wg3)):
                            sp.dma_start(to, A["Wg"][n * D:(n + 1) * D, :]).then_inc(s_wg, 16)
                        sp.wait_ge(s_wg, 2 * 16)

                @block.scalar
                def _(act):
                    def step_act(i):
                        for s in range(NS):
                            wait(act, s_T[s], i)
                            nc.scalar.copy(stage[s], cols(SUM, (i * NS + s) * P, P)).then_inc(s_stage[s], 1)
                    loop(act, NT // NS, step_act)

                @block.tensor
                def _(pe):
                    if not onto_x:
                        pe.wait_ge(s_diff, 1)
                    def step_pe(i):
                        for s in range(NS):
                            wait(pe, s_stage[s], i + 1)
                            wait(pe, s_copied[s], i)
                            if not onto_x:
                                nc.tensor.matmul(psum[s][:, P:P + 1], stage[s], wg_agg, start=True, stop=True)
                            nc.tensor.transpose(psum[s][:, 0:P], stage[s], ident[:, :]).then_inc(s_T[s], 1)
                    loop(pe, NT // NS, step_pe)

                @block.vector
                def _(dve):
                    if not onto_x:
                        dve.wait_ge(s_wg, 2 * 16)
                        nc.vector.tensor_tensor(wg_agg, wg2, wg3, ALU.subtract).then_inc(s_diff, 1)
                    def step_dve(i):
                        for s in range(NS):
                            wait(dve, s_T[s], i + 1)
                            if onto_x:
                                x = X[:, bass.ds(i * NS + s, 1), :].rearrange("p a d -> p (a d)")
                                nc.vector.tensor_tensor(x, x, psum[s][:, 0:P], ALU.add).then_inc(s_copied[s], 1)
                            else:
                                nc.vector.tensor_copy(cols(z_agg, i * NS + s, 1), psum[s][:, P:P + 1])
                                nc.vector.tensor_copy(cols(SUM, (i * NS + s) * P, P), psum[s][:, 0:P]).then_inc(s_copied[s], 1)
                    loop(dve, NT // NS, step_dve)

        def gate_and_norm():
            n = max(n for n in range(1, NT) if NT % n == 0 and 2 * n * D <= SCR.shape[1] * 2 // 3)
            CH = NT // n
            U = max(u for u in range(1, 6) if n % u == 0)
            carve = Carve()
            tmp = [carve(n * D) for _ in range(2)]
            wg, gamma, beta = carve(3 * D), carve(D), carve(D)
            z, dev, var, mean, scale, shift = (carve(NT) for _ in range(6))
            stats = carve(6 * NT)
            alpha, neg_bg = carve(1), carve(1)
            skip = W[:, 0:NP]
            s_load, s_chain, s_wg, s_prod, s_dot, s_diff, s_z, s_e, s_var, s_std, s_affine, s_norm, s_scaled, s_rst, s_x = (
                sem(f"g_{x}") for x in ("load", "chain", "wg", "prod", "dot", "diff", "z", "e", "var", "std",
                                        "affine", "norm", "scaled", "rst", "x"))
            s_stats = sem("g_stats")
            t3 = lambda t: t.rearrange("p (t d) -> p t d", d=D)
            over = lambda row: row.unsqueeze(1).broadcast_to([P, n, D])
            spread = lambda col: col.unsqueeze(2).broadcast_to([P, n, D])
            tiles = lambda c: slice(c * n, (c + 1) * n)
            columns = lambda c: slice(c * n * D, (c + 1) * n * D)
            with nc.Block() as block:
                @block.sync
                def _(sp):
                    for to, of in ((wg, A["Wg"].rearrange("n a -> (n a)")), (gamma, A["gamma"]), (beta, A["beta"]), (alpha, A["alpha"]), (neg_bg, A["bg"])):
                        sp.dma_start(to, of.partition_broadcast(P)).then_inc(s_load, 16)
                    sp.dma_start(t3(skip), ks_table[:, D:2 * D].rearrange("(t p) d -> p t d", p=P)).then_inc(s_load, 16)
                    sp.wait_ge(s_load, 6 * 16)

                @block.gpsimd
                def _(pool):
                    pt = nc.gpsimd.tensor_tensor
                    wg_skip = wg[:, 0:D]
                    def front(c):
                        if c >= 2:
                            pool.wait_ge(s_dot, c - 1)
                        pt(t3(tmp[c % 2]), t3(skip[:, columns(c)]), over(wg_skip), ALU.mult).then_inc(s_prod, 1)
                        pool.wait_ge(s_prod, c + 1)
                        pt(skip[:, columns(c)], skip[:, columns(c)], SUM[:, columns(c)], ALU.subtract).then_inc(s_diff, 1)

                    def scaled(c):
                        rows = t3(SUM[:, columns(c)])
                        pool.wait_ge(s_norm, (c + 1) * n)
                        pt(rows, rows, over(gamma), ALU.mult).then_inc(s_scaled, 1)

                    def onto_x(c):
                        rows = SUM[:, columns(c)]
                        pool.wait_ge(s_rst, c + 1)
                        x = X[:, tiles(c), :].rearrange("p t d -> p (t d)")
                        pt(x, x, rows, ALU.add).then_inc(s_x, 1)

                    pool.wait_ge(s_wg, 1)
                    front(0)
                    front(1)
                    for c in range(CH):
                        scaled(c)
                        if c + 2 < CH:
                            front(c + 2)
                        onto_x(c)

                @block.scalar
                def _(act):
                    def gate(c):
                        act.wait_ge(s_z, c + 1)
                        nc.scalar.activation(z[:, tiles(c)], z[:, tiles(c)], ACT.Exp, scale=-1.0).then_inc(s_e, 1)

                    gate(0)
                    for c in range(CH):
                        act.wait_ge(s_var, c + 1)
                        nc.scalar.activation(var[:, tiles(c)], var[:, tiles(c)], ACT.Sqrt).then_inc(s_std, 1)
                        act.wait_ge(s_affine, c + 1)
                        with act.Fori(c * n // U, (c + 1) * n // U) as i:
                            for j in range(U):
                                t = i * U + j
                                rows = cols(SUM, t * D, D)
                                nc.scalar.activation(rows, rows, ACT.Identity, bias=cols(shift, t, 1), scale=cols(scale, t, 1)).then_inc(s_norm, 1)
                        if c + 1 < CH:
                            gate(c + 1)

                @block.vector
                def _(dve):
                    link, v = chained(dve, s_chain), nc.vector
                    dve.wait_ge(s_load, 6 * 16)
                    v.tensor_tensor(wg[:, 0:D], wg[:, 0:D], wg[:, 2 * D:3 * D], ALU.add).then_inc(s_wg, 1)

                    def dots(c):
                        ts = tiles(c)
                        dve.wait_ge(s_prod, c + 1)
                        v.tensor_reduce(z[:, ts], t3(tmp[c % 2]), AX, ALU.add).then_inc(s_dot, 1)
                        dve.wait_ge(s_dot, c + 1)
                        v.scalar_tensor_tensor(z[:, ts], z[:, ts], neg_bg, z_agg[:, ts], ALU.add, ALU.add).then_inc(s_z, 1)

                    def front(c):
                        ts, rows, diff = tiles(c), SUM[:, columns(c)], skip[:, columns(c)]
                        dve.wait_ge(s_e, c + 1)
                        link(v.tensor_scalar(z[:, ts], z[:, ts], 1.0, None, ALU.add))
                        link(v.reciprocal(z[:, ts], z[:, ts]))
                        dve.wait_ge(s_diff, c + 1)
                        link(v.tensor_tensor(t3(diff), t3(diff), spread(z[:, ts]), ALU.mult))
                        link(v.tensor_tensor(rows, rows, diff, ALU.add))
                        with dve.Fori(c * n // U, (c + 1) * n // U) as i:
                            for j in range(U):
                                v.bn_stats(cols(stats, (i * U + j) * 6, 6), cols(SUM, (i * U + j) * D, D)).then_inc(s_stats, 1)
                        dve.wait_ge(s_stats, (c + 1) * n)
                        st = stats.rearrange("p (t k) -> p t k", k=6)[:, ts, :]
                        moments(link, st, mean[:, ts], dev[:, ts], var[:, ts], s_var)
                        dve.wait_ge(s_std, c + 1)
                        link(v.reciprocal(scale[:, ts], var[:, ts]))
                        v.scalar_tensor_tensor(shift[:, ts], mean[:, ts], -1.0, scale[:, ts], ALU.mult, ALU.mult).then_inc(s_affine, 1)

                    def back(c):
                        rows, low = SUM[:, columns(c)], skip[:, columns(c)]
                        dve.wait_ge(s_scaled, c + 1)
                        link(v.tensor_tensor(t3(rows), t3(rows), over(beta), ALU.add))
                        link(v.tensor_scalar(low, rows, 0.0, alpha, ALU.min, ALU.mult))
                        v.scalar_tensor_tensor(rows, rows, 0.0, low, ALU.max, ALU.add).then_inc(s_rst, 1)

                    dots(0)
                    for c in range(CH + 1):
                        if c < CH:
                            front(c)
                        if c + 1 < CH:
                            dots(c + 1)
                        if c:
                            back(c - 1)

        def store():
            s_stored = sem("o_stored")
            whole, rest = n_nodes // P, n_nodes % P
            with nc.Block() as block:
                @block.sync
                def _(sp):
                    sp.dma_start(A["out"][0:whole * P, :].rearrange("(t p) d -> p t d", p=P), X[:, 0:whole, :]).then_inc(s_stored, 16)
                    if rest:
                        sp.dma_start(A["out"][whole * P:n_nodes, :], X[0:rest, whole, :]).then_inc(s_stored, 16)
                    sp.wait_ge(s_stored, 16 * (2 if rest else 1))

        phase(setup)
        phase(node_tables, 0)
        phase(pass_a, 0)
        phase(edge_softmax, "s0", [W1], float(HD) ** -0.5)
        phase(pass_b, 0)
        phase(sums_to_rows, "r0", False)
        phase(gate_and_norm)
        phase(node_tables, 1)
        phase(pass_a, 1)
        phase(edge_softmax, "s1", [W1, W2], 1.0)
        phase(pass_b, 1)
        phase(sums_to_rows, "r1", True)
        phase(store)


def kernel(x, src, dst, edge_attr_128, L0_gnn_Wq, L0_gnn_bq, L0_gnn_Wk, L0_gnn_bk, L0_gnn_Wv, L0_gnn_bv,
           L0_gnn_Ws, L0_gnn_bs, L0_gnn_Wg, L0_gnn_bg, L0_gnn_gamma, L0_gnn_beta, L0_gnn_alpha,
           L1_gnn_W_src, L1_gnn_W_dst, L1_gnn_W_edge, L1_gnn_attn_src, L1_gnn_attn_dst, L1_gnn_attn_edge):
    import concourse.bacc as bacc
    from concourse.bass_utils import run_bass_kernel_spmd

    n_nodes, n_edges = x.shape[0], src.shape[0]
    NT, ET = sizes(n_nodes, n_edges)
    ep = ET * P
    f = lambda a: np.asarray(a)
    x_pad = np.zeros((NT * P, D), np.float32)
    x_pad[:n_nodes] = f(x)
    src_pad = np.zeros(ep, np.int32)
    src_pad[:n_edges] = f(src)
    dst_line = np.full(ep + 2, -1, np.int32)
    dst_line[1:n_edges + 1] = f(dst)
    dst_line[n_edges + 1:ep + 1] = n_nodes
    dst_pad = dst_line[1:-1]
    xe_T = np.zeros((D, ep), np.float32)
    xe_T[:, :n_edges] = f(edge_attr_128).T
    arrays = {
        "x": x_pad, "xe_T": xe_T, "dst_line": dst_line,
        "src_tiles": src_pad.reshape(ET, P).T, "dst_tiles": dst_pad.reshape(ET, P).T,
        "tile_first": dst_pad.reshape(ET, P)[:, 0].reshape(1, ET),
        "Wq": f(L0_gnn_Wq), "Wk": f(L0_gnn_Wk), "Wv": f(L0_gnn_Wv), "Ws": f(L0_gnn_Ws),
        "bq": f(L0_gnn_bq), "bk": f(L0_gnn_bk), "bv": f(L0_gnn_bv), "bs": f(L0_gnn_bs),
        "Wg": f(L0_gnn_Wg), "bg": f(L0_gnn_bg), "gamma": f(L0_gnn_gamma), "beta": f(L0_gnn_beta),
        "alpha": f(L0_gnn_alpha).reshape(1),
        "W_src": f(L1_gnn_W_src), "W_src_T": f(L1_gnn_W_src).T, "W_dst": f(L1_gnn_W_dst), "W_dst_T": f(L1_gnn_W_dst).T, "W_edge": f(L1_gnn_W_edge), "W_edge_T": f(L1_gnn_W_edge).T,
        "attn_src": f(L1_gnn_attn_src), "attn_dst": f(L1_gnn_attn_dst), "attn_edge": f(L1_gnn_attn_edge),
    }
    nc = bacc.Bacc("TRN2", target_bir_lowering=False, num_devices=1)
    ins, A = {}, {}
    for name, a in arrays.items():
        a = np.ascontiguousarray(a)
        ins[f"in_{name}"] = a
        A[name] = nc.dram_tensor(f"in_{name}", a.shape, mybir.dt.from_np(a.dtype), kind="ExternalInput").ap()
    A["out"] = nc.dram_tensor("out", (n_nodes, D), F32, kind="ExternalOutput").ap()
    build(nc, A, n_nodes, n_edges)
    r = run_bass_kernel_spmd(nc, [ins], core_ids=[0])
    return r.results[0]["out"]
```
